# Optimizing a Trainium2 kernel written in Bass

```python
import numpy as np
import jax
import jax.numpy as jnp

def _softmax(x, axis=-1):
    return jax.nn.softmax(x, axis=axis)

def _gelu(x):
    return jax.nn.gelu(x, approximate=True)

def _silu(x):
    return jax.nn.silu(x)

def _sigmoid(x):
    return jax.nn.sigmoid(x)

def _layernorm(x, axis=-1, eps=1e-05):
    m = jnp.mean(x, axis=axis, keepdims=True)
    v = jnp.var(x, axis=axis, keepdims=True)
    return (x - m) / jnp.sqrt(v + eps)

def _scatter_add(tgt, idx, src, axis=0):
    return tgt.at[idx].add(src)

def _segment_sum(src, seg, n):
    return jax.ops.segment_sum(src, seg, n)
kernel_name = 'mk_xattn_ffn_d1_seqx_r4_ad1975'

def setup_inputs(seed: int=0):
    np.random.seed(seed)
    _w = jnp.asarray

    def _rec_inputs():
        import jax
        import jax.numpy as jnp
        _rk = jax.random.key(seed)
        x = -0.0003929 + 0.9999 * jax.random.normal(jax.random.fold_in(_rk, 1), (8, 512, 256), jnp.float32)
        _lenS = 512 - jax.random.randint(jax.random.fold_in(_rk, 7), (8,), 0, max(1, 512 // 4) + 1, jnp.int32)
        _lenS2 = 1024 - jax.random.randint(jax.random.fold_in(_rk, 8), (8,), 0, max(1, 1024 // 4) + 1, jnp.int32)
        _ctx_1024P = jax.random.normal(jax.random.fold_in(_rk, 11), (8, 16, 256), jnp.float32)
        _ctx_1024c = jax.random.dirichlet(jax.random.fold_in(_rk, 511), 0.3 * jnp.ones((16,), jnp.float32), (8, 1024))
        _ctx_1024t = jnp.einsum('bsk,bkd->bsd', _ctx_1024c, _ctx_1024P)
        _ctx_1024t = _ctx_1024t * jax.lax.rsqrt(jnp.mean(jnp.square(_ctx_1024t)) + 1e-12) * 0.953939
        ctx_1024 = 0.00208318 + 0.999174 * (_ctx_1024t + 0.3 * jax.random.normal(jax.random.fold_in(_rk, 611), (8, 1024, 256), jnp.float32))
        _validS = jnp.arange(512)[None, :] < _lenS[:, None]
        _validS2 = jnp.arange(1024)[None, :] < _lenS2[:, None]
        _causal = jnp.tril(jnp.ones((512, 512), dtype=bool))
        mask_BxSxS2_ff0 = jnp.where(jnp.ones((8, 512, 1024), dtype=bool), 0.0, -1000000000.0).astype(jnp.float32)
        return (x, ctx_1024, mask_BxSxS2_ff0)
    x, ctx_1024, mask_BxSxS2_ff0 = _rec_inputs()

    def _L0_xattn_setup():
        import jax, jax.numpy as jnp
        import numpy as np
        NUM_HEADS = 16
        DIM = 256
        key = jax.random.key(seed)
        ks = jax.random.split(key, 12)
        B, N, T, C = (4, 1024, 77, DIM)
        s = 1.0 / np.sqrt(C)
        return {'hidden_states': jax.random.normal(ks[0], (B, N, C), jnp.float32), 'encoder_hidden_states': jax.random.normal(ks[1], (B, T, C), jnp.float32), 'attention_mask': jnp.zeros((B, N, T), jnp.float32), 'Wq': jax.random.normal(ks[2], (C, C), jnp.float32) * s, 'bq': jnp.zeros((C,), jnp.float32), 'Wk': jax.random.normal(ks[3], (C, C), jnp.float32) * s, 'bk': jnp.zeros((C,), jnp.float32), 'Wv': jax.random.normal(ks[4], (C, C), jnp.float32) * s, 'bv': jnp.zeros((C,), jnp.float32), 'Wo': jax.random.normal(ks[5], (C, C), jnp.float32) * s, 'bo': jnp.zeros((C,), jnp.float32)}
    _L0_xattn_all = _L0_xattn_setup()
    _L0_xattn_in = {k: v for k, v in _L0_xattn_all.items() if k in ('Wq', 'bq', 'Wk', 'bk', 'Wv', 'bv', 'Wo', 'bo')}
    del _L0_xattn_all

    def _L0_ffn_setup():
        import jax, jax.numpy as jnp
        import numpy as np

        def _binarize(w):
            alpha = jax.lax.stop_gradient(jnp.mean(jnp.abs(w), axis=1, keepdims=True))
            bw = alpha * jnp.sign(w)
            return w + jax.lax.stop_gradient(bw - w)
        key = jax.random.key(seed)
        k1, k2, k3, k4, k5 = jax.random.split(key, 5)
        D, H = (256, 1024)
        x = jax.random.normal(k1, (64, 196, D), dtype=jnp.float32)
        w1 = jax.random.normal(k2, (H, D), dtype=jnp.float32) * 0.02
        b1 = jax.random.normal(k3, (H,), dtype=jnp.float32) * 0.02
        w2 = jax.random.normal(k4, (D, H), dtype=jnp.float32) * 0.02
        b2 = jax.random.normal(k5, (D,), dtype=jnp.float32) * 0.02
        return {'x': x, 'w1': w1, 'b1': b1, 'w2': w2, 'b2': b2}
    _L0_ffn_all = _L0_ffn_setup()
    _L0_ffn_in = {k: v for k, v in _L0_ffn_all.items() if k in ('w1', 'b1', 'w2', 'b2')}
    del _L0_ffn_all
    return {'x': x, 'ctx_1024': ctx_1024, 'mask_BxSxS2_ff0': mask_BxSxS2_ff0, 'L0_xattn_Wq': _L0_xattn_in['Wq'], 'L0_xattn_bq': _L0_xattn_in['bq'], 'L0_xattn_Wk': _L0_xattn_in['Wk'], 'L0_xattn_bk': _L0_xattn_in['bk'], 'L0_xattn_Wv': _L0_xattn_in['Wv'], 'L0_xattn_bv': _L0_xattn_in['bv'], 'L0_xattn_Wo': _L0_xattn_in['Wo'], 'L0_xattn_bo': _L0_xattn_in['bo'], 'L0_ffn_w1': _L0_ffn_in['w1'], 'L0_ffn_b1': _L0_ffn_in['b1'], 'L0_ffn_w2': _L0_ffn_in['w2'], 'L0_ffn_b2': _L0_ffn_in['b2']}

def reference(x, ctx_1024, mask_BxSxS2_ff0, L0_xattn_Wq, L0_xattn_bq, L0_xattn_Wk, L0_xattn_bk, L0_xattn_Wv, L0_xattn_bv, L0_xattn_Wo, L0_xattn_bo, L0_ffn_w1, L0_ffn_b1, L0_ffn_w2, L0_ffn_b2):
    import jax
    import jax.numpy as jnp

    def _L0_xattn_ref(hidden_states, encoder_hidden_states, attention_mask, Wq, bq, Wk, bk, Wv, bv, Wo, bo):
        import jax, jax.numpy as jnp
        import numpy as np
        NUM_HEADS = 16
        DIM = 256
        B, N, C = hidden_states.shape
        T = encoder_hidden_states.shape[1]
        H = NUM_HEADS
        D = C // H
        q = (hidden_states @ Wq.T + bq).reshape(B, N, H, D).transpose(0, 2, 1, 3)
        k = (encoder_hidden_states @ Wk.T + bk).reshape(B, T, H, D).transpose(0, 2, 1, 3)
        v = (encoder_hidden_states @ Wv.T + bv).reshape(B, T, H, D).transpose(0, 2, 1, 3)
        scale = 1.0 / jnp.sqrt(jnp.asarray(D, q.dtype))
        scores = jnp.einsum('bhnd,bhtd->bhnt', q, k) * scale + attention_mask[:, None, :, :]
        attn = jax.nn.softmax(scores, axis=-1)
        out = jnp.einsum('bhnt,bhtd->bhnd', attn, v)
        out = out.transpose(0, 2, 1, 3).reshape(B, N, C)
        return out @ Wo.T + bo

    def _L0_ffn_ref(x, w1, b1, w2, b2):
        import jax, jax.numpy as jnp
        import numpy as np

        def _binarize(w):
            alpha = jax.lax.stop_gradient(jnp.mean(jnp.abs(w), axis=1, keepdims=True))
            bw = alpha * jnp.sign(w)
            return w + jax.lax.stop_gradient(bw - w)
        bw1 = _binarize(w1)
        h = jnp.einsum('bsd,hd->bsh', x, bw1) + b1
        h = jax.nn.gelu(h, approximate=False)
        bw2 = _binarize(w2)
        out = jnp.einsum('bsh,dh->bsd', h, bw2) + b2
        return out
    x = x + _L0_xattn_ref(_layernorm(x, axis=-1), ctx_1024, mask_BxSxS2_ff0, L0_xattn_Wq, L0_xattn_bq, L0_xattn_Wk, L0_xattn_bk, L0_xattn_Wv, L0_xattn_bv, L0_xattn_Wo, L0_xattn_bo)
    x = x + _L0_ffn_ref(_layernorm(x, axis=-1), L0_ffn_w1, L0_ffn_b1, L0_ffn_w2, L0_ffn_b2)
    return x

_drawn_inputs = setup_inputs


def setup_inputs(seed=0):
    import zlib

    import numpy as np

    out = dict(_drawn_inputs(seed))
    spreads = {'L0_xattn_bq': (0.0, 0.401),
     'L0_xattn_bk': (0.0, 0.8),
     'L0_xattn_bv': (0.0, 0.1),
     'L0_xattn_bo': (0.0, 0.1)}
    factors = {'L0_ffn_b1': 8.0, 'L0_ffn_b2': 3.356}
    for name, (base, spread) in spreads.items():
        noise = np.random.default_rng([zlib.crc32(name.encode()), seed]).standard_normal(out[name].shape)
        drawn = base * np.exp(spread * noise) if base else spread * noise
        out[name] = jnp.asarray(drawn.astype(out[name].dtype))
    for name, factor in factors.items():
        out[name] = (out[name] * factor).astype(out[name].dtype)
    return out
```

```python
import numpy as np
import concourse.bass as bass
from concourse import mybir
from contextlib import ExitStack

F32 = mybir.dt.float32
F32R = mybir.dt.float32r
I32 = mybir.dt.int32
ALU = mybir.AluOpType
ACT = mybir.ActivationFunctionType
AX = mybir.AxisListType

P = 128
NB, S, T, D = 8, 512, 1024, 256
NH, DH, HID = 16, 16, 1024
CT = D // P
ST = S // P
KC = T // P
HC = HID // P
NG = 4
GH = NH // NG
NPAIR = NH // 2
SCALE = 0.25
EPS = 1e-5
SUM_LO, SUM_HI = 2.0 ** -30, 2.0 ** 30

A_USES = 6
B_USES = 2 * NG * KC
X_USES = 2 * NH * ST
M_READY, M_FREE = 12, 6
T_READY, T_FREE = 5, 3
STACK = 16 * 16


def layer(nc, x, ctx_t, mask, wq_t, wk_t, wv_t, wo_t, bq, bk, bv_row, bo_row, w1, w1_t, w2_t, b1, b2_row,
          ident_in, halves_in, out):
    es = ExitStack()
    with es:
        def sb(name, shape, dt=F32):
            return es.enter_context(nc.sbuf_tensor(name, shape, dt))

        def sem(name):
            return es.enter_context(nc.semaphore(name))

        ident = sb("ident", [P, P])
        halves = sb("halves", [P, 2])
        zero = sb("zero", [P, 1])
        mean_w = sb("mean_w", [P, P])
        wq, wk, wv, wo = (sb(n, [P, CT, D]) for n in ("wq", "wk", "wv", "wo"))
        w1_sign = sb("w1_sign", [P, CT, HID], F32R)
        w2_sign = sb("w2_sign", [P, HC, D], F32R)
        bq_s, bk_s = sb("bq_s", [P, CT]), sb("bk_s", [P, CT])
        b1_s, alpha1 = sb("b1_s", [P, HC]), sb("alpha1", [P, HC])
        bv_s, bo_s, b2_s, alpha2 = (sb(n, [P, D]) for n in ("bv_s", "bo_s", "b2_s", "alpha2"))
        stage = sb("stage", [P, ST, T])
        w1t_raw = stage[:, 0:2, :]
        w2t_raw = stage[:, 2:4, :]
        ctx_s = sb("ctx_s", [P, CT, T])
        xn = sb("xn", [P, ST, D])
        xnT = sb("xnT", [P, CT, S])
        q_split = sb("q_split", [P, 2, CT, S])
        k_split = sb("k_split", [P, 2, CT, T])
        probsT = k_split[:].rearrange("p a t (b n) -> p (a t b) n", n=S)
        q_stack = sb("q_stack", [P, NPAIR, S], F32R)
        k_stack = sb("k_stack", [P, NPAIR, T], F32R)
        v_aug = sb("v_aug", [P, KC, 2, NH // 2, 32])
        probs = sb("probs", [P, 4, T])
        attn_e, attn_o = sb("attn_e", [P, S]), sb("attn_o", [P, S])
        sums, rsum, attn_u = sb("sums", [P, S]), sb("rsum", [P, S]), sb("attn_u", [P, S])
        attnT = sb("attnT", [P, CT, S])
        y = sb("y", [P, ST, D])
        xn2 = sb("xn2", [P, ST, D])
        xh, xl = sb("xh", [P, CT, S], F32R), sb("xl", [P, CT, S], F32R)
        hf = sb("hf", [P, 2, S])
        hh, hl = sb("hh", [P, 2, S], F32R), sb("hl", [P, 2, S], F32R)
        bn, mv = sb("bn", [P, ST, 6]), sb("mv", [P, ST, 2])
        var, rstd, minus_half = sb("var", [P, ST]), sb("rstd", [P, ST]), sb("minus_half", [P, ST])
        row_max = sb("row_max", [P, 1])
        found = sb("found", [P, NB, 8])
        small = sb("small", [P, 5])
        bad, bad2, bad_all, dve_idle, pool_idle = (small[:, k:k + 1] for k in range(5))
        flag = sb("flag", [P, 1], I32)

        slot = [es.enter_context(nc.psum_tensor(f"slot{i}", [P, 2 * S], F32)) for i in range(2)]
        acc = [es.enter_context(nc.psum_tensor(f"acc{i}", [P, S], F32)) for i in range(2)]
        bank = [es.enter_context(nc.psum_tensor(f"bank{i}", [P, S], F32)) for i in range(2)]

        x0_loaded, w_loaded, wv_loaded = sem("x0_loaded"), sem("w_loaded"), sem("wv_loaded")
        const_loaded, ffn_loaded = sem("const_loaded"), sem("ffn_loaded")
        x_loaded, ctx_loaded, res_loaded = sem("x_loaded"), sem("ctx_loaded"), sem("res_loaded")
        mask_loaded, mask_used = sem("mask_loaded"), sem("mask_used")
        mean_w_set, exponent_set, abs_ready, signs_ready = sem("mean_w_set"), sem("exponent_set"), sem("abs_ready"), sem("signs_ready")
        var_ready, rstd_ready = sem("var_ready"), sem("rstd_ready")
        xn_ready, xn2_ready = sem("xn_ready"), sem("xn2_ready")
        stack_ready = [sem(f"stack_ready{p}") for p in range(NPAIR)]
        slot_ready, slot_free = sem("slot_ready"), [sem("slot0_free"), sem("slot1_free")]
        acc_ready, acc_free = sem("acc_ready"), [sem("acc0_free"), sem("acc1_free")]
        bank_ready, bank_free = sem("bank_ready"), [sem("bank0_free"), sem("bank1_free")]
        attn_ready, h_split, out_ready, out_stored = sem("attn_ready"), sem("h_split"), sem("out_ready"), sem("out_stored")
        pool_ticks = sem("pool_ticks")
        max_ready, exact_probs = sem("max_ready"), sem("exact_probs")
        dve_done, bad_ready, bad_summed, flag_ready = sem("dve_done"), sem("bad_ready"), sem("bad_summed"), sem("flag_ready")

        block = es.enter_context(nc.Block())

        @block.sync
        def _(sp):
            sp.dma_start(wq[:], wq_t).then_inc(w_loaded, 16)
            sp.dma_start(wk[:], wk_t).then_inc(w_loaded, 16)
            sp.dma_start(wv[:], wv_t).then_inc(wv_loaded, 16)
            sp.dma_start(bv_s[:], bv_row).then_inc(wv_loaded, 16)
            sp.dma_start(stage[:, 2:4, :].rearrange("p a n -> p (a n)"), w2_t).then_inc(ffn_loaded, 16)
            sp.dma_start(probs[:, 2:4, :].rearrange("p a n -> p (a n)"), w1).then_inc(ffn_loaded, 16)
            sp.dma_start(stage[:, 0:2, :], w1_t).then_inc(ffn_loaded, 16)
            sp.dma_start(b1_s[:], b1).then_inc(ffn_loaded, 16)
            sp.dma_start(wo[:], wo_t).then_inc(ffn_loaded, 16)
            sp.dma_start(bo_s[:], bo_row).then_inc(ffn_loaded, 16)
            sp.dma_start(b2_s[:], b2_row).then_inc(ffn_loaded, 16)

            def build_stacks(freed):
                sp.wait_ge(slot_free[0], freed + 2)
                sp.wait_ge(slot_free[1], freed + 2)
                for p in range(NPAIR):
                    for a in range(2):
                        t, row = divmod((2 * p + a) * DH, P)
                        for r in range(4):
                            to = slice(64 * a + 16 * r, 64 * a + 16 * r + DH)
                            sp.dma_start(q_stack[to, p, :].bitcast(F32),
                                         q_split[row:row + DH, r // 2, t, :]).then_inc(stack_ready[p], 16)
                            sp.dma_start(k_stack[to, p, :].bitcast(F32),
                                         k_split[row:row + DH, r % 2, t, :]).then_inc(stack_ready[p], 16)

            build_stacks(0)
            with sp.Fori(0, NB - 1) as n:
                build_stacks((A_USES + B_USES) // 2 * n + (A_USES + B_USES) // 2)
            sp.wait_ge(flag_ready, 1)
            with sp.If(sp.value_load(flag[0:1, 0:1]) != 0):
                with sp.Fori(0, NB) as i:
                    build_stacks((A_USES + X_USES) // 2 * i + (A_USES + B_USES) // 2 * NB)

        @block.gpsimd
        def _(pool):
            pool.dma_start(xn[:], x[0].rearrange("(m p) c -> p m c", p=P)).then_inc(x_loaded, 16)
            pool.dma_start(ident[:], ident_in).then_inc(x0_loaded, 16)
            pool.dma_start(ctx_s[:], ctx_t[0].rearrange("(t p) n -> p t n", p=P)).then_inc(ctx_loaded, 16)
            pool.dma_start(bq_s[:], bq).then_inc(const_loaded, 16)
            pool.dma_start(bk_s[:], bk).then_inc(const_loaded, 16)
            pool.dma_start(halves[:], halves_in).then_inc(const_loaded, 16)
            nc.gpsimd.memset(minus_half[:], -0.5).then_inc(exponent_set, 1)
            pool.wait_ge(exponent_set, 1)

            def hold(semaphore, value, ticks):
                if not (isinstance(ticks, int) and ticks == 0):
                    pool.wait_ge(pool_ticks, ticks)
                pool.wait_ge(semaphore, value)
                nc.gpsimd.tensor_tensor(pool_idle, minus_half[:, 0:1], minus_half[:, 0:1], ALU.mult
                                        ).then_inc(pool_ticks, 1)

            def power(k):
                pool.wait_ge(var_ready, k)
                nc.gpsimd.tensor_tensor(rstd[:], var[:], minus_half[:], ALU.pow).then_inc(rstd_ready, 1)

            def store(b, n, ticks):
                hold(out_ready, 2 * n + 2, ticks)
                pool.dma_start(out[b].rearrange("(m p) c -> p m c", p=P), xn2[:]).then_inc(out_stored, 16)
                hold(out_stored, 16 * n + 16, ticks + 1)

            def mask_part(b, n, part):
                pool.dma_start(stage[:, 0:2, :],
                               mask[b, part * 2 * P:(part + 1) * 2 * P, :].rearrange("(m p) k -> p m k", p=P)
                               ).then_inc(mask_loaded, 16)

            def batch(n, last):
                pool.dma_start(y[:], x[n].rearrange("(m p) c -> p m c", p=P)).then_inc(res_loaded, 16)
                if not last:
                    hold(slot_ready, (A_USES + B_USES) * n + A_USES, 4 * n + 1)
                    pool.dma_start(xn[:], x[n + 1].rearrange("(m p) c -> p m c", p=P)).then_inc(x_loaded, 16)
                    pool.dma_start(ctx_s[:], ctx_t[n + 1].rearrange("(t p) n -> p t n", p=P)).then_inc(ctx_loaded, 16)
                mask_part(n, n, 0)
                hold(mask_used, 2 * n + 1, 4 * n + (1 if last else 2))
                mask_part(n, n, 1)
                if not last:
                    power(2 * n + 2)
                    power(2 * n + 3)
                else:
                    power(2 * n + 2)
                store(n, n, 4 * n + (2 if last else 3))

            hold(exponent_set, 1, 0)
            power(1)
            pool.wait_ge(signs_ready, 1)
            with pool.Fori(0, NB - 1) as n:
                batch(n, False)
            batch(NB - 1, True)
            pool.wait_ge(flag_ready, 1)
            with pool.If(pool.value_load(flag[0:1, 0:1]) != 0):
                with pool.Fori(0, NB) as i:
                    pool.dma_start(xn[:], x[i].rearrange("(m p) c -> p m c", p=P)).then_inc(x_loaded, 16)
                    pool.dma_start(ctx_s[:], ctx_t[i].rearrange("(t p) n -> p t n", p=P)).then_inc(ctx_loaded, 16)
                    pool.dma_start(y[:], x[i].rearrange("(m p) c -> p m c", p=P)).then_inc(res_loaded, 16)
                    pool.dma_start(stage[:], mask[i].rearrange("(m p) k -> p m k", p=P)).then_inc(mask_loaded, 16)
                    power(2 * i + 2 * NB + 1)
                    power(2 * i + 2 * NB + 2)
                    store(i, i + NB, 2 * i + 4 * NB)

        @block.tensor
        def _(pe):
            def stage_a(n, used, freed, first=False):
                pe.wait_ge(xn_ready, n + 1)
                if not first:
                    pe.wait_ge(slot_free[0], freed)
                for c in range(CT):
                    for m in range(ST):
                        last = nc.tensor.transpose(slot[0][:, c * S + m * P:c * S + (m + 1) * P],
                                                   xn[:, m, c * P:(c + 1) * P], ident[:])
                last.then_inc(slot_ready, 1)
                if first:
                    pe.wait_ge(w_loaded, 32)
                else:
                    pe.wait_ge(slot_free[1], freed)
                pe.wait_ge(slot_free[0], freed + 1)
                for t in range(CT):
                    for c in range(CT):
                        last = nc.tensor.matmul(slot[1][:, t * S:(t + 1) * S], wq[:, c, t * P:(t + 1) * P],
                                                xnT[:, c, :], start=(c == 0), stop=(c == CT - 1))
                last.then_inc(slot_ready, 1)
                pe.wait_ge(ctx_loaded, 16 * n + 16)
                for t in range(CT):
                    if t == 1:
                        pe.wait_ge(slot_free[1], freed + 1)
                    for half in range(2):
                        for c in range(CT):
                            last = nc.tensor.matmul(slot[t][:, half * S:(half + 1) * S], wk[:, c, t * P:(t + 1) * P],
                                                    ctx_s[:, c, half * S:(half + 1) * S],
                                                    start=(c == 0), stop=(c == CT - 1))
                    last.then_inc(slot_ready, 1)
                if first:
                    pe.wait_ge(wv_loaded, 32)
                for v in range(2):
                    pe.wait_ge(slot_free[v], freed + 2)
                    for kk in range(KC // 2):
                        kc = v * (KC // 2) + kk
                        for c in range(CT):
                            last = nc.tensor.matmul(slot[v][:, kk * D:(kk + 1) * D], ctx_s[:, c, kc * P:(kc + 1) * P],
                                                    wv[:, c, :], start=(c == 0), stop=(c == CT - 1))
                    last.then_inc(slot_ready, 1)

            def values(n, j):
                g, kc = divmod(j, KC)
                if kc == 0:
                    pe.wait_ge(acc_free[g % 2], T_FREE * n + g // 2 + 1)
                for h in range(GH):
                    e = 2 * j + h // 2
                    last = nc.tensor.matmul(acc[g % 2][32 * h:32 * h + 32, :], v_aug[:, kc, g % 2, (g // 2) * GH + h, :],
                                            probs[:, e % 4, (h % 2) * S:(h % 2 + 1) * S],
                                            start=(kc == 0), stop=(kc == KC - 1))
                if kc == KC - 1:
                    last.then_inc(acc_ready, 1)

            def stage_b(n, freed):
                for j in range(NG * KC):
                    g, kc = divmod(j, KC)
                    for i in range(2):
                        p = 2 * g + i
                        if kc == 0:
                            pe.wait_ge(stack_ready[p], STACK * n + STACK)
                        pe.wait_ge(slot_free[i], freed + j)
                        for a in range(2):
                            last = nc.tensor.matmul(slot[i][:, a * S:(a + 1) * S],
                                                    k_stack[64 * a:64 * a + 64, p, kc * P:(kc + 1) * P],
                                                    q_stack[64 * a:64 * a + 64, p, :], start=True, stop=True)
                        last.then_inc(slot_ready, 1)
                    if j:
                        values(n, j - 1)
                for i in range(2):
                    pe.wait_ge(slot_free[i], freed + NG * KC)
                values(n, NG * KC - 1)

            def exact_b(n, i, freed):
                for hd in range(NH):
                    g, h = divmod(hd, GH)
                    p, a = divmod(hd, 2)
                    if a == 0:
                        pe.wait_ge(stack_ready[p], STACK * n + STACK)
                    for qi in range(ST):
                        k = hd * ST + qi
                        pe.wait_ge(slot_free[0], freed + k)
                        for half in range(2):
                            last = nc.tensor.matmul(slot[0][:, half * S:(half + 1) * S],
                                                    q_stack[64 * a:64 * a + 64, p, qi * P:(qi + 1) * P],
                                                    k_stack[64 * a:64 * a + 64, p, half * S:(half + 1) * S],
                                                    start=True, stop=True)
                        last.then_inc(slot_ready, 1)
                        pe.wait_ge(exact_probs, NH * ST * i + k + 1)
                        pe.wait_ge(slot_free[1], freed + k)
                        for kc in range(KC):
                            last = nc.tensor.transpose(slot[1][:, kc * P:(kc + 1) * P],
                                                       probs[:, 1, kc * P:(kc + 1) * P], ident[:])
                        last.then_inc(slot_ready, 1)
                    pe.wait_ge(slot_free[1], freed + (hd + 1) * ST)
                    if h == 0:
                        pe.wait_ge(acc_free[g % 2], T_FREE * n + g // 2 + 1)
                    for kc in range(KC):
                        last = nc.tensor.matmul(acc[g % 2][32 * h:32 * h + 32, :], v_aug[:, kc, g % 2, (g // 2) * GH + h, :],
                                                probsT[:, kc, :], start=(kc == 0), stop=(kc == KC - 1))
                    if h == GH - 1:
                        last.then_inc(acc_ready, 1)

            def stage_o(n):
                pe.wait_ge(attn_ready, 2 * n + 2)
                for m in range(ST):
                    if m % 2 == 0:
                        pe.wait_ge(bank_free[m // 2], M_FREE * n + 1)
                    for c in range(CT):
                        last = nc.tensor.matmul(bank[m // 2][:, (m % 2) * D:(m % 2 + 1) * D],
                                                attnT[:, c, m * P:(m + 1) * P], wo[:, c, :],
                                                start=(c == 0), stop=(c == CT - 1))
                    if m % 2:
                        last.then_inc(bank_ready, 1)

            def stage_f(n):
                pe.wait_ge(xn2_ready, n + 1)
                for c in range(CT):
                    pe.wait_ge(bank_free[c], M_FREE * n + 2)
                    for m in range(ST):
                        last = nc.tensor.transpose(bank[c][:, m * P:(m + 1) * P], xn2[:, m, c * P:(c + 1) * P], ident[:])
                    last.then_inc(bank_ready, 1)
                for c in range(CT):
                    pe.wait_ge(bank_free[c], M_FREE * n + 3)

                def up(m):
                    if m >= 2:
                        pe.wait_ge(bank_free[m % 2], M_FREE * n + 3 + m // 2)
                    k = 0
                    for part in (xh, xl):
                        for c in range(CT):
                            last = nc.tensor.matmul(bank[m % 2][:], w1_sign[:, c, m * P:(m + 1) * P], part[:, c, :],
                                                    start=(k == 0), stop=(k == 2 * CT - 1))
                            k += 1
                    last.then_inc(bank_ready, 1)

                up(0)
                up(1)
                for a in range(2):
                    pe.wait_ge(acc_free[a], T_FREE * n + 3)
                for m in range(HC):
                    pe.wait_ge(h_split, HC * n + m + 1)
                    for tok in range(ST):
                        for part in (hh, hl):
                            first = m == 0 and tok % 2 == 0 and part is hh
                            done = m == HC - 1 and tok % 2 == 1 and part is hl
                            last = nc.tensor.matmul(acc[tok // 2][:, (tok % 2) * D:(tok % 2 + 1) * D],
                                                    part[:, m % 2, tok * P:(tok + 1) * P], w2_sign[:, m, :],
                                                    start=first, stop=done, skip_group_check=True)
                    if m == HC - 1:
                        last.then_inc(acc_ready, 1)
                    if m + 2 < HC:
                        up(m + 2)

            pe.wait_ge(x0_loaded, 16)
            stage_a(0, 0, 0, first=True)
            pe.wait_ge(mean_w_set, 1)
            pe.wait_ge(abs_ready, 1)
            for half in range(2):
                for m in range(HC):
                    last = nc.tensor.matmul(bank[half][:, 0:P], mean_w[:],
                                            probs[:, 0:2, :].rearrange("p a (b d) -> p (a b) d", d=D)[:, m, half * P:(half + 1) * P],
                                            start=(m == 0), stop=(m == HC - 1))
                last.then_inc(bank_ready, 1)
            pe.wait_ge(signs_ready, 1)
            per = A_USES + B_USES
            with pe.Fori(0, NB - 1) as n:
                stage_b(n, per // 2 * n + A_USES // 2)
                stage_o(n)
                stage_a(n + 1, per * n + per, per // 2 * n + per // 2)
                stage_f(n)
            stage_b(NB - 1, per // 2 * (NB - 1) + A_USES // 2)
            stage_o(NB - 1)
            stage_f(NB - 1)
            pe.wait_ge(bad_ready, 1)
            nc.tensor.matmul(bank[0][:, 0:1], mean_w[:], bad, start=True, stop=True).then_inc(bad_summed, 1)
            pe.wait_ge(flag_ready, 1)
            with pe.If(pe.value_load(flag[0:1, 0:1]) != 0):
                per_x = A_USES + X_USES
                with pe.Fori(0, NB) as i:
                    stage_a(i + NB, per_x * i + per * NB, per_x // 2 * i + per // 2 * NB)
                    exact_b(i + NB, i, per_x // 2 * i + (per // 2 * NB + A_USES // 2))
                    stage_o(i + NB)
                    stage_f(i + NB)

        @block.scalar
        def _(act):
            def stage_a(used):
                act.wait_ge(slot_ready, used + 1)
                nc.scalar.copy(xnT[:].rearrange("p c n -> p (c n)"), slot[0][:]).then_inc(slot_free[0], 1)

            def stage_b(used):
                for e in range(B_USES):
                    act.wait_ge(slot_ready, used + e + 1)
                    nc.scalar.activation(probs[:, e % 4, :], slot[e % 2][:], ACT.Exp, scale=SCALE
                                         ).then_inc(slot_free[e % 2], 1)

            def exact_b(i):
                for k in range(NH * ST):
                    act.wait_ge(max_ready, NH * ST * i + k + 1)
                    nc.scalar.activation(probs[:, 1, :], probs[:, 0, :], ACT.Exp, bias=row_max[:, 0:1]
                                         ).then_inc(exact_probs, 1)

            def stage_f(n):
                for m in range(HC):
                    act.wait_ge(bank_ready, M_READY * n + 2 + 5 + m)
                    if m >= 2:
                        act.wait_ge(h_split, HC * n + m - 1)
                    nc.scalar.activation(hf[:, m % 2, :], bank[m % 2][:], ACT.Gelu, bias=b1_s[:, m:m + 1],
                                         scale=alpha1[:, m:m + 1]).then_inc(bank_free[m % 2], 1)

            act.wait_ge(ffn_loaded, 16 * 7)
            nc.scalar.activation(probs[:, 0:2, :], w2t_raw, ACT.Abs).then_inc(abs_ready, 1)
            stage_a(0)
            act.wait_ge(signs_ready, 1)
            per = A_USES + B_USES
            with act.Fori(0, NB - 1) as n:
                stage_b(per * n + A_USES)
                stage_a(per * n + per)
                stage_f(n)
            stage_b(per * (NB - 1) + A_USES)
            stage_f(NB - 1)
            act.wait_ge(flag_ready, 1)
            with act.If(act.value_load(flag[0:1, 0:1]) != 0):
                with act.Fori(0, NB) as i:
                    stage_a((A_USES + X_USES) * i + per * NB)
                    exact_b(i)
                    stage_f(i + NB)

        @block.vector
        def _(dve):
            chain = [0, 0]

            def done(ins):
                ins.then_inc(dve_done, 1)
                chain[1] += 1
                return chain[0] + chain[1]

            def counted_loop(times, per_pass, body):
                start = chain[0] + chain[1]
                with dve.Fori(0, times) as i:
                    chain[0], chain[1] = per_pass * i + start, 0
                    body(i)
                    assert chain[1] == per_pass, chain[1]
                chain[0], chain[1] = start + times * per_pass, 0

            def statistics(src, k):
                for m in range(ST):
                    c = done(nc.vector.bn_stats(bn[:, m, :], src[:, m, :]))
                dve.wait_ge(dve_done, c)
                nc.vector.memset(dve_idle, 0.0)
                for m in range(ST):
                    c = done(nc.vector.bn_aggr(mv[:, m, :], bn[:, m, :]))
                dve.wait_ge(dve_done, c)
                nc.vector.tensor_scalar(var[:], mv[:, :, 1], EPS, None, ALU.add).then_inc(var_ready, 1)
                dve.wait_ge(rstd_ready, k)

            def layernorm(dst, src, k, ready):
                statistics(src, k)
                for m in range(ST):
                    last = nc.vector.tensor_scalar(dst[:, m, :], src[:, m, :], mv[:, m, 0:1], rstd[:, m:m + 1],
                                                   ALU.subtract, ALU.mult)
                last.then_inc(ready, 1)

            def norm_x(n, k):
                dve.wait_ge(x_loaded, 16 * n + 16)
                layernorm(xn, xn, k, xn_ready)

            def split(hi, lo, src, bias, signal):
                c = done(nc.vector.tensor_scalar(hi.bitcast(F32R), src, bias, None, ALU.add))
                dve.wait_ge(dve_done, c)
                last = nc.vector.scalar_tensor_tensor(lo.bitcast(F32R), src, bias, hi, ALU.add, ALU.subtract)
                if signal is None:
                    done(last)
                else:
                    last.then_inc(signal, 1)

            def stage_a(used):
                dve.wait_ge(slot_ready, used + 2)
                for t in range(CT):
                    split(q_split[:, 0, t, :], q_split[:, 1, t, :], slot[1][:, t * S:(t + 1) * S], bq_s[:, t:t + 1],
                          slot_free[1] if t == CT - 1 else None)
                for t in range(CT):
                    dve.wait_ge(slot_ready, used + 3 + t)
                    split(k_split[:, 0, t, :], k_split[:, 1, t, :], slot[t][:], bk_s[:, t:t + 1], slot_free[t])
                for v in range(2):
                    dve.wait_ge(slot_ready, used + 5 + v)
                    for e in range(2):
                        last = nc.vector.tensor_tensor(
                            v_aug[:, v * (KC // 2):(v + 1) * (KC // 2), e, :, 16 * e:16 * e + DH],
                            slot[v][:].rearrange("p (k e h d) -> p k e h d", e=2, h=NH // 2, d=DH)[:, :, e, :, :],
                            bv_s[:].rearrange("p (e h d) -> p e h d", e=2, d=DH)[:, e, :, :].unsqueeze(1)
                            .to_broadcast([P, KC // 2, NH // 2, DH]), ALU.add)
                    last.then_inc(slot_free[v], 1)

            def count_mask(n):
                for part in range(2):
                    dve.wait_ge(mask_loaded, 32 * n + 16 * (part + 1))
                    nc.vector.tensor_scalar(stage[:, 0:2, :], stage[:, 0:2, :], 0.0, None, ALU.not_equal, ALU.add,
                                            accum_out=found[:, n, part:part + 1]).then_inc(mask_used, 1)

            def residual(n):
                dve.wait_ge(res_loaded, 16 * n + 16)
                done(nc.vector.tensor_tensor(y[:], y[:], bo_s[:].unsqueeze(1).to_broadcast([P, ST, D]), ALU.add))

            def take_even(n, t):
                dve.wait_ge(acc_ready, T_READY * n + 2 * t + 1)
                nc.vector.tensor_copy(attn_e[:], acc[0][:]).then_inc(acc_free[0], 1)

            def take_odd(n, t, check):
                dve.wait_ge(acc_ready, T_READY * n + 2 * t + 2)
                nc.vector.tensor_copy(attn_o[:], acc[1][:]).then_inc(acc_free[1], 1)
                dve.wait_ge(acc_free[0], T_FREE * n + t + 2)
                c = done(nc.vector.tensor_scalar(sums[:], attn_e[:], halves[:, 1:2], None, ALU.mult))
                dve.wait_ge(dve_done, c)
                dve.wait_ge(acc_free[1], T_FREE * n + t + 2)
                c = done(nc.vector.scalar_tensor_tensor(sums[:], attn_o[:], halves[:, 0:1], sums[:], ALU.mult, ALU.add))
                dve.wait_ge(dve_done, c)
                if check is not None:
                    for k, (op, bound) in enumerate(((ALU.min, SUM_HI), (ALU.max, SUM_LO))):
                        c = done(nc.vector.scalar_tensor_tensor(rsum[:], sums[:], bound, sums[:], op, ALU.is_equal,
                                                                accum_out=found[:, check, 2 + 3 * t + k:3 + 3 * t + k]))
                        dve.wait_ge(dve_done, c)
                c = done(nc.vector.reciprocal(sums[:], sums[:]))
                c = done(nc.vector.tensor_scalar(attn_u[:], attn_e[:], halves[:, 0:1], None, ALU.mult))
                dve.wait_ge(dve_done, c)
                c = done(nc.vector.scalar_tensor_tensor(attn_u[:], attn_o[:], halves[:, 1:2], attn_u[:], ALU.mult, ALU.add))
                c = done(nc.vector.stream_shuffle(rsum[:], sums[:], list(range(16, 32)) + list(range(16))))
                dve.wait_ge(dve_done, c)
                if check is not None:
                    c = done(nc.vector.scalar_tensor_tensor(sums[:], attn_u[:], 0.0, zero[:].to_broadcast([P, S]), ALU.mult, ALU.is_equal,
                                                            accum_out=found[:, check, 4 + 3 * t:5 + 3 * t]))
                nc.vector.tensor_tensor(attnT[:, t, :], attn_u[:], rsum[:], ALU.mult).then_inc(attn_ready, 1)

            def stage_o(n, k):
                for a in range(2):
                    dve.wait_ge(bank_ready, M_READY * n + 2 + 1 + a)
                    yy = y[:, 2 * a:2 * a + 2, :].rearrange("p m c -> p (m c)")
                    nc.vector.tensor_tensor(yy, bank[a][:], yy, ALU.add).then_inc(bank_free[a], 1)
                for a in range(2):
                    dve.wait_ge(bank_free[a], M_FREE * n + 2)
                layernorm(xn2, y, k, xn2_ready)
                dve.wait_ge(xn2_ready, n + 1)
                c = done(nc.vector.tensor_tensor(y[:], y[:], b2_s[:].unsqueeze(1).to_broadcast([P, ST, D]), ALU.add))
                return c

            def stage_f(n, y_ready):
                for c in range(CT):
                    dve.wait_ge(bank_ready, M_READY * n + 2 + 3 + c)
                    d = done(nc.vector.tensor_copy(xh[:, c, :], bank[c][:]))
                    dve.wait_ge(dve_done, d)
                    nc.vector.tensor_tensor(xl[:, c, :], bank[c][:], xh[:, c, :].bitcast(F32), ALU.subtract
                                            ).then_inc(bank_free[c], 1)
                for m in range(HC):
                    dve.wait_ge(bank_free[m % 2], M_FREE * n + 4 + m // 2)
                    d = done(nc.vector.tensor_copy(hh[:, m % 2, :], hf[:, m % 2, :]))
                    dve.wait_ge(dve_done, d)
                    nc.vector.tensor_tensor(hl[:, m % 2, :], hf[:, m % 2, :], hh[:, m % 2, :].bitcast(F32), ALU.subtract
                                            ).then_inc(h_split, 1)
                dve.wait_ge(dve_done, y_ready)
                dve.wait_ge(acc_ready, T_READY * n + 5)
                for a in range(2):
                    to = xn2[:, 2 * a:2 * a + 2, :]
                    nc.vector.tensor_tensor(to, acc[a][:].rearrange("p (m c) -> p m c", c=D),
                                            alpha2[:].unsqueeze(1).to_broadcast([P, 2, D]), ALU.mult
                                            ).then_inc(acc_free[a], 1)
                    dve.wait_ge(acc_free[a], T_FREE * n + 4)
                    nc.vector.tensor_tensor(to, to, y[:, 2 * a:2 * a + 2, :], ALU.add).then_inc(out_ready, 1)

            nc.vector.memset(mean_w[:], 1.0 / HID).then_inc(mean_w_set, 1)
            done(nc.vector.memset(zero[:], 0.0))
            nc.vector.memset(v_aug[:, :, 0, :, 16:32], 1.0).then_inc(acc_free[0], 1)
            nc.vector.memset(v_aug[:, :, 1, :, 0:16], 1.0).then_inc(acc_free[1], 1)
            norm_x(0, 1)
            dve.wait_ge(const_loaded, 48)
            dve.wait_ge(wv_loaded, 32)
            stage_a(0)
            dve.wait_ge(ffn_loaded, 16 * 7)
            c = done(nc.vector.tensor_reduce(alpha1[:], probs[:, 2:4, :].rearrange("p a (b d) -> p (a b) d", d=D),
                                             AX.X, ALU.add, apply_absolute_value=True))
            dve.wait_ge(dve_done, c)
            done(nc.vector.tensor_scalar(alpha1[:], alpha1[:], 1.0 / D, None, ALU.mult))
            k_tmp = attnT[:].rearrange("p c n -> p (c n)")
            for raw, sign in ((w1t_raw.rearrange("p a n -> p (a n)"), w1_sign[:].rearrange("p a n -> p (a n)")),
                              (w2t_raw.rearrange("p a n -> p (a n)"), w2_sign[:].rearrange("p a n -> p (a n)"))):
                for half in range(2):
                    part = slice(half * T, (half + 1) * T)
                    c = done(nc.vector.tensor_scalar(k_tmp, raw[:, part], 0.0, None, ALU.is_lt))
                    dve.wait_ge(dve_done, c)
                    c = done(nc.vector.scalar_tensor_tensor(sign[:, part], raw[:, part], 0.0, k_tmp, ALU.is_gt, ALU.subtract))
                    dve.wait_ge(dve_done, c)
            for half in range(2):
                dve.wait_ge(bank_ready, half + 1)
                nc.vector.tensor_copy(alpha2[:, half * P:(half + 1) * P], bank[half][:, 0:P]).then_inc(bank_free[half], 1)
                dve.wait_ge(bank_free[half], 1)
            nc.vector.memset(row_max[:], 0.0).then_inc(signs_ready, 1)

            def fast_batch(n, last):
                residual(n)
                count_mask(n)
                if not last:
                    norm_x(n + 1, 2 * n + 2)
                for t in range(CT):
                    take_even(n, t)
                    take_odd(n, t, n)
                y_ready = stage_o(n, 2 * n + (2 if last else 3))
                if not last:
                    stage_a((A_USES + B_USES) * n + (A_USES + B_USES))
                stage_f(n, y_ready)

            counted_loop(NB - 1, FAST_DONE, lambda n: fast_batch(n, False))
            fast_batch(NB - 1, True)

            mask_found = found[:, :, 0:2]
            good_found = found[:, :, 2:8]
            c = done(nc.vector.tensor_reduce(bad, mask_found, AX.XY, ALU.add))
            c = done(nc.vector.tensor_reduce(bad2, good_found, AX.XY, ALU.add))
            dve.wait_ge(dve_done, c)
            c = done(nc.vector.tensor_scalar(bad2, bad2, -1.0, float(NB * 6 * S), ALU.mult, ALU.add))
            dve.wait_ge(dve_done, c)
            nc.vector.tensor_tensor(bad, bad, bad2, ALU.add).then_inc(bad_ready, 1)
            dve.wait_ge(bad_summed, 1)
            c = done(nc.vector.tensor_scalar(bad_all, bank[0][:, 0:1], 0.0, None, ALU.not_equal))
            dve.wait_ge(dve_done, c)
            nc.vector.tensor_copy(flag[:], bad_all).then_inc(flag_ready, 1)
            dve.wait_ge(flag_ready, 1)

            def exact_batch(i):
                n = i + NB
                norm_x(n, 2 * i + 2 * NB + 1)
                stage_a((A_USES + X_USES) * i + (A_USES + B_USES) * NB)
                residual(n)
                dve.wait_ge(mask_loaded, 16 * i + 32 * NB + 16)
                for p in range(NPAIR):
                    dve.wait_ge(stack_ready[p], STACK * n + STACK)
                used = (A_USES + X_USES) * i + ((A_USES + B_USES) * NB + A_USES)
                for hd in range(NH):
                    for qi in range(ST):
                        k = hd * ST + qi
                        dve.wait_ge(slot_ready, used + 2 * k + 1)
                        nc.vector.scalar_tensor_tensor(probs[:, 0, :], slot[0][:], SCALE, stage[:, qi, :],
                                                       ALU.mult, ALU.add).then_inc(slot_free[0], 1)
                        dve.wait_ge(slot_free[0], (A_USES + X_USES) // 2 * i
                                    + ((A_USES + B_USES) // 2 * NB + A_USES // 2 + k + 1))
                        nc.vector.tensor_reduce(row_max[:], probs[:, 0, :], AX.X, ALU.max, negate=True
                                                ).then_inc(max_ready, 1)
                        dve.wait_ge(slot_ready, used + 2 * k + 2)
                        nc.vector.tensor_copy(probsT[:, :, qi * P:(qi + 1) * P],
                                              slot[1][:].rearrange("p (k q) -> p k q", q=P)).then_inc(slot_free[1], 1)
                    g, h = divmod(hd, GH)
                    if h == GH - 1:
                        if g % 2 == 0:
                            take_even(n, g // 2)
                        else:
                            take_odd(n, g // 2, None)
                y_ready = stage_o(n, 2 * i + 2 * NB + 2)
                stage_f(n, y_ready)

            with dve.If(dve.value_load(flag[0:1, 0:1]) != 0):
                counted_loop(NB, EXACT_DONE, exact_batch)


FAST_DONE, EXACT_DONE = 51, 45


def _rows(w):
    return np.ascontiguousarray(w.reshape(-1, P, w.shape[1]).transpose(1, 0, 2))


def kernel(**inputs):
    import concourse.bacc as _bacc
    from concourse.bass_utils import run_bass_kernel_spmd as _run

    a = {k: np.asarray(v) for k, v in inputs.items()}
    f = lambda name: a["L0_" + name]
    tile, col, par, ch = np.meshgrid(np.arange(2), np.arange(4), np.arange(2), np.arange(DH), indexing="ij")
    attn_order = (DH * (GH * (2 * tile + par) + col) + ch).reshape(-1)
    par, half, col, ch = np.meshgrid(np.arange(2), np.arange(2), np.arange(4), np.arange(DH), indexing="ij")
    v_order = (DH * (GH * (2 * half + par) + col) + ch).reshape(-1)
    row = lambda v: np.ascontiguousarray(np.broadcast_to(v[None, :], (P, v.shape[0])))
    col_ = lambda v: np.ascontiguousarray(v.reshape(-1, P).T)
    w1, w2 = f("ffn_w1"), f("ffn_w2")
    lane = np.arange(P) % 32 < 16
    arrays = {
        "x": a["x"], "ctx_t": np.ascontiguousarray(a["ctx_1024"].transpose(0, 2, 1)), "mask": a["mask_BxSxS2_ff0"],
        "wq_t": _rows(f("xattn_Wq").T), "wk_t": _rows(f("xattn_Wk").T), "wv_t": _rows(f("xattn_Wv").T[:, v_order]),
        "wo_t": _rows(f("xattn_Wo").T[attn_order]), "bq": col_(f("xattn_bq")), "bk": col_(f("xattn_bk")),
        "bv_row": row(f("xattn_bv")[v_order]), "bo_row": row(f("xattn_bo")),
        "w1": _rows(w1).reshape(P, -1), "w1_t": _rows(w1.T), "w2_t": _rows(w2.T).reshape(P, -1),
        "b1": col_(f("ffn_b1")), "b2_row": row(f("ffn_b2")),
        "ident": np.eye(P, dtype=np.float32), "halves": np.stack([lane, ~lane], 1).astype(np.float32),
    }
    nc = _bacc.Bacc("TRN2", target_bir_lowering=False, num_devices=1)
    args = [nc.dram_tensor("in_" + n, v.shape, F32, kind="ExternalInput").ap() for n, v in arrays.items()]
    out = nc.dram_tensor("out", (NB, S, D), F32, kind="ExternalOutput").ap()
    layer(nc, *args, out)
    r = _run(nc, [{"in_" + n: v for n, v in arrays.items()}], core_ids=[0])
    return r.results[0]["out"]
```

```python
import numpy as np
import concourse.bass as bass
from concourse import mybir
from contextlib import ExitStack

F32 = mybir.dt.float32
F32R = mybir.dt.float32r
I32 = mybir.dt.int32
ALU = mybir.AluOpType
ACT = mybir.ActivationFunctionType
AX = mybir.AxisListType

P = 128
NB, S, T, D = 8, 512, 1024, 256
NH, DH, HID = 16, 16, 1024
CT = D // P
ST = S // P
KC = T // P
HC = HID // P
NG = 4
GH = NH // NG
NPAIR = NH // 2
QRING = 4
SCALE = 0.25
EPS = 1e-5
SUM_LO, SUM_HI = 2.0 ** -30, 2.0 ** 30

A_USES = 6
B_USES = 2 * NG * KC
X_USES = 2 * NH * ST
M_READY, M_FREE = 12, 6
T_READY, T_FREE = 5, 3
STACK = 8 * 16


def layer(nc, x, ctx_t, mask, wq_t, wk_t, wv_t, wo_t, bq, bk, bv_row, bo_row, w1, w1_t, w2_t, b1, b2_row,
          ident_in, halves_in, out):
    es = ExitStack()
    with es:
        def sb(name, shape, dt=F32):
            return es.enter_context(nc.sbuf_tensor(name, shape, dt))

        def sem(name):
            return es.enter_context(nc.semaphore(name))

        ident = sb("ident", [P, P])
        halves = sb("halves", [P, 2])
        zero = sb("zero", [P, 1])
        mean_w = sb("mean_w", [P, P])
        wq, wk, wv, wo = (sb(n, [P, CT, D]) for n in ("wq", "wk", "wv", "wo"))
        w1_sign = sb("w1_sign", [P, CT, HID], F32R)
        w2_sign = sb("w2_sign", [P, HC, D], F32R)
        bq_s, bk_s = sb("bq_s", [P, CT]), sb("bk_s", [P, CT])
        b1_s, alpha1 = sb("b1_s", [P, HC]), sb("alpha1", [P, HC])
        bv_s, bo_s, b2_s, alpha2 = (sb(n, [P, D]) for n in ("bv_s", "bo_s", "b2_s", "alpha2"))
        stage = sb("stage", [P, 2, T])
        ctx_s = sb("ctx_s", [P, CT, T])
        xn = sb("xn", [P, ST, D])
        xnT = sb("xnT", [P, CT, S])
        q_split = sb("q_split", [P, 2, CT, S])
        k_split = sb("k_split", [P, 2, CT, T])
        probsT = k_split[:].rearrange("p a t (b n) -> p (a t b) n", n=S)
        q_stack = sb("q_stack", [P, NPAIR, S])
        q_head = sb("q_head", [P, QRING, 2, S], F32R)
        k_stack = sb("k_stack", [P, NPAIR, T], F32R)
        v_aug = sb("v_aug", [P, KC, 2, NH // 2, 32])
        probs = sb("probs", [P, 4, T])
        w2t_raw, w1_raw = probs[:, 0:2, :], probs[:, 2:4, :]
        sums = sb("sums", [P, S])
        attnT = sb("attnT", [P, CT, S])
        y = sb("y", [P, ST, D])
        xn2 = sb("xn2", [P, ST, D])
        xh, xl = sb("xh", [P, CT, S], F32R), sb("xl", [P, CT, S], F32R)
        hf = sb("hf", [P, 2, S])
        attn_e, attn_o = hf[:, 0, :], hf[:, 1, :]
        xn2_halves = xn2[:].rearrange("p (a m) c -> p a (m c)", a=2)
        rsum, attn_u = xn2_halves[:, 0, :], xn2_halves[:, 1, :]
        hh, hl = sb("hh", [P, 2, S], F32R), sb("hl", [P, 2, S], F32R)
        bn, mv = sb("bn", [P, ST, 6]), sb("mv", [P, ST, 2])
        var, rstd, minus_half = sb("var", [P, ST]), sb("rstd", [P, ST]), sb("minus_half", [P, ST])
        row_max = sb("row_max", [P, 1])
        found = sb("found", [P, NB, 8])
        small = sb("small", [P, 5])
        bad, bad2, bad_all, dve_idle, pool_idle = (small[:, k:k + 1] for k in range(5))
        flag = sb("flag", [P, 1], I32)

        slot = [es.enter_context(nc.psum_tensor(f"slot{i}", [P, 2 * S], F32)) for i in range(2)]
        acc = [es.enter_context(nc.psum_tensor(f"acc{i}", [P, S], F32)) for i in range(2)]
        bank = [es.enter_context(nc.psum_tensor(f"bank{i}", [P, S], F32)) for i in range(2)]

        x0_loaded, w_loaded, wv_loaded = sem("x0_loaded"), sem("w_loaded"), sem("wv_loaded")
        const_loaded, ffn_loaded = sem("const_loaded"), sem("ffn_loaded")
        x_loaded, ctx_loaded, res_loaded = sem("x_loaded"), sem("ctx_loaded"), sem("res_loaded")
        mask_loaded, mask_used = sem("mask_loaded"), sem("mask_used")
        mean_w_set, exponent_set, abs_ready, signs_ready = sem("mean_w_set"), sem("exponent_set"), sem("abs_ready"), sem("signs_ready")
        var_ready, rstd_ready = sem("var_ready"), sem("rstd_ready")
        xn_ready, xn2_ready = sem("xn_ready"), sem("xn2_ready")
        stack_ready = [sem(f"stack_ready{p}") for p in range(NPAIR)]
        slot_ready, slot_free = sem("slot_ready"), [sem("slot0_free"), sem("slot1_free")]
        acc_ready, acc_free = sem("acc_ready"), [sem("acc0_free"), sem("acc1_free")]
        bank_ready, bank_free = sem("bank_ready"), [sem("bank0_free"), sem("bank1_free")]
        attn_ready, h_split, out_ready, out_stored = sem("attn_ready"), sem("h_split"), sem("out_ready"), sem("out_stored")
        pool_ticks = sem("pool_ticks")
        q_masked, xh_ready = sem("q_masked"), sem("xh_ready")
        max_ready, exact_probs = sem("max_ready"), sem("exact_probs")
        dve_done, bad_ready, bad_summed, flag_ready = sem("dve_done"), sem("bad_ready"), sem("bad_summed"), sem("flag_ready")

        block = es.enter_context(nc.Block())

        @block.sync
        def _(sp):
            sp.dma_start(wq[:], wq_t).then_inc(w_loaded, 16)
            sp.dma_start(wk[:], wk_t).then_inc(w_loaded, 16)
            sp.dma_start(wv[:], wv_t).then_inc(wv_loaded, 16)
            sp.dma_start(bv_s[:], bv_row).then_inc(wv_loaded, 16)
            sp.dma_start(w2t_raw.rearrange("p a n -> p (a n)"), w2_t).then_inc(ffn_loaded, 16)
            sp.dma_start(w1_raw.rearrange("p a n -> p (a n)"), w1).then_inc(ffn_loaded, 16)
            sp.dma_start(stage[:], w1_t).then_inc(ffn_loaded, 16)
            sp.dma_start(b1_s[:], b1).then_inc(ffn_loaded, 16)
            sp.dma_start(wo[:], wo_t).then_inc(ffn_loaded, 16)
            sp.dma_start(bo_s[:], bo_row).then_inc(ffn_loaded, 16)
            sp.dma_start(b2_s[:], b2_row).then_inc(ffn_loaded, 16)

            def build_stacks(freed):
                sp.wait_ge(slot_free[0], freed + 2)
                sp.wait_ge(slot_free[1], freed + 2)
                for p in range(NPAIR):
                    t, row = divmod(2 * DH * p, P)
                    for r in range(4):
                        to = slice(32 * r, 32 * r + 2 * DH)
                        sp.dma_start(q_stack[to, p, :], q_split[row:row + 2 * DH, r // 2, t, :]).then_inc(stack_ready[p], 16)
                        sp.dma_start(k_stack[to, p, :].bitcast(F32),
                                     k_split[row:row + 2 * DH, r % 2, t, :]).then_inc(stack_ready[p], 16)

            build_stacks(0)
            with sp.Fori(0, NB - 1) as n:
                build_stacks((A_USES + B_USES) // 2 * n + (A_USES + B_USES) // 2)
            sp.wait_ge(flag_ready, 1)
            with sp.If(sp.value_load(flag[0:1, 0:1]) != 0):
                with sp.Fori(0, NB) as i:
                    build_stacks((A_USES + X_USES) // 2 * i + (A_USES + B_USES) // 2 * NB)

        @block.gpsimd
        def _(pool):
            pool.dma_start(xn[:], x[0].rearrange("(m p) c -> p m c", p=P)).then_inc(x_loaded, 16)
            pool.dma_start(ident[:], ident_in).then_inc(x0_loaded, 16)
            pool.dma_start(ctx_s[:], ctx_t[0].rearrange("(t p) n -> p t n", p=P)).then_inc(ctx_loaded, 16)
            pool.dma_start(bq_s[:], bq).then_inc(const_loaded, 16)
            pool.dma_start(bk_s[:], bk).then_inc(const_loaded, 16)
            pool.dma_start(halves[:], halves_in).then_inc(const_loaded, 16)
            nc.gpsimd.memset(minus_half[:], -0.5).then_inc(exponent_set, 1)
            pool.wait_ge(exponent_set, 1)

            def hold(semaphore, value, ticks):
                if not (isinstance(ticks, int) and ticks == 0):
                    pool.wait_ge(pool_ticks, ticks)
                pool.wait_ge(semaphore, value)
                nc.gpsimd.tensor_tensor(pool_idle, minus_half[:, 0:1], minus_half[:, 0:1], ALU.mult
                                        ).then_inc(pool_ticks, 1)

            def power(k):
                pool.wait_ge(var_ready, k)
                nc.gpsimd.tensor_tensor(rstd[:], var[:], minus_half[:], ALU.pow).then_inc(rstd_ready, 1)

            def store(b, n, ticks):
                hold(out_ready, 2 * n + 2, ticks)
                pool.dma_start(out[b].rearrange("(m p) c -> p m c", p=P), xn2[:]).then_inc(out_stored, 16)
                hold(out_stored, 16 * n + 16, ticks + 1)

            def mask_part(b, n, part):
                pool.dma_start(stage[:],
                               mask[b, part * 2 * P:(part + 1) * 2 * P, :].rearrange("(m p) k -> p m k", p=P)
                               ).then_inc(mask_loaded, 16)

            def batch(n, last):
                pool.dma_start(y[:], x[n].rearrange("(m p) c -> p m c", p=P)).then_inc(res_loaded, 16)
                if not last:
                    hold(slot_ready, (A_USES + B_USES) * n + A_USES, 4 * n + 1)
                    pool.dma_start(xn[:], x[n + 1].rearrange("(m p) c -> p m c", p=P)).then_inc(x_loaded, 16)
                    pool.dma_start(ctx_s[:], ctx_t[n + 1].rearrange("(t p) n -> p t n", p=P)).then_inc(ctx_loaded, 16)
                mask_part(n, n, 0)
                hold(mask_used, 2 * n + 1, 4 * n + (1 if last else 2))
                mask_part(n, n, 1)
                if not last:
                    power(2 * n + 2)
                    power(2 * n + 3)
                else:
                    power(2 * n + 2)
                store(n, n, 4 * n + (2 if last else 3))

            hold(exponent_set, 1, 0)
            power(1)
            pool.wait_ge(signs_ready, 1)
            with pool.Fori(0, NB - 1) as n:
                batch(n, False)
            batch(NB - 1, True)
            pool.wait_ge(flag_ready, 1)
            with pool.If(pool.value_load(flag[0:1, 0:1]) != 0):
                with pool.Fori(0, NB) as i:
                    pool.dma_start(xn[:], x[i].rearrange("(m p) c -> p m c", p=P)).then_inc(x_loaded, 16)
                    pool.dma_start(ctx_s[:], ctx_t[i].rearrange("(t p) n -> p t n", p=P)).then_inc(ctx_loaded, 16)
                    pool.dma_start(y[:], x[i].rearrange("(m p) c -> p m c", p=P)).then_inc(res_loaded, 16)
                    for half, to in enumerate((stage[:], probs[:, 2:4, :])):
                        pool.dma_start(to, mask[i, 2 * half * P:2 * (half + 1) * P, :].rearrange("(m p) k -> p m k", p=P)
                                       ).then_inc(mask_loaded, 16)
                    power(2 * i + 2 * NB + 1)
                    power(2 * i + 2 * NB + 2)
                    store(i, i + NB, 2 * i + 4 * NB)

        @block.tensor
        def _(pe):
            def stage_a(n, freed, first=False):
                pe.wait_ge(xn_ready, n + 1)
                if not first:
                    pe.wait_ge(slot_free[0], freed)
                for c in range(CT):
                    for m in range(ST):
                        last = nc.tensor.transpose(slot[0][:, c * S + m * P:c * S + (m + 1) * P],
                                                   xn[:, m, c * P:(c + 1) * P], ident[:])
                last.then_inc(slot_ready, 1)
                if first:
                    pe.wait_ge(w_loaded, 32)
                else:
                    pe.wait_ge(slot_free[1], freed)
                pe.wait_ge(slot_free[0], freed + 1)
                for t in range(CT):
                    for c in range(CT):
                        last = nc.tensor.matmul(slot[1][:, t * S:(t + 1) * S], wq[:, c, t * P:(t + 1) * P],
                                                xnT[:, c, :], start=(c == 0), stop=(c == CT - 1))
                last.then_inc(slot_ready, 1)
                pe.wait_ge(ctx_loaded, 16 * n + 16)
                for t in range(CT):
                    if t == 1:
                        pe.wait_ge(slot_free[1], freed + 1)
                    for half in range(2):
                        for c in range(CT):
                            last = nc.tensor.matmul(slot[t][:, half * S:(half + 1) * S], wk[:, c, t * P:(t + 1) * P],
                                                    ctx_s[:, c, half * S:(half + 1) * S],
                                                    start=(c == 0), stop=(c == CT - 1))
                    last.then_inc(slot_ready, 1)

            def stage_v(freed, first=False):
                if first:
                    pe.wait_ge(wv_loaded, 32)
                for v in range(2):
                    pe.wait_ge(slot_free[v], freed + 2)
                    for kk in range(KC // 2):
                        kc = v * (KC // 2) + kk
                        for c in range(CT):
                            last = nc.tensor.matmul(slot[v][:, kk * D:(kk + 1) * D], ctx_s[:, c, kc * P:(kc + 1) * P],
                                                    wv[:, c, :], start=(c == 0), stop=(c == CT - 1))
                    last.then_inc(slot_ready, 1)

            def values(n, j):
                g, kc = divmod(j, KC)
                if kc == 0:
                    pe.wait_ge(acc_free[g % 2], T_FREE * n + g // 2 + 1)
                for h in range(GH):
                    e = 2 * j + h // 2
                    last = nc.tensor.matmul(acc[g % 2][32 * h:32 * h + 32, :], v_aug[:, kc, g % 2, (g // 2) * GH + h, :],
                                            probs[:, e % 4, (h % 2) * S:(h % 2 + 1) * S],
                                            start=(kc == 0), stop=(kc == KC - 1))
                if kc == KC - 1:
                    last.then_inc(acc_ready, 1)

            def stage_b(n, freed):
                for j in range(NG * KC):
                    g, kc = divmod(j, KC)
                    for i in range(2):
                        p = 2 * g + i
                        if kc == 0:
                            pe.wait_ge(q_masked, 2 * NPAIR * n + 2 * p + 2)
                        pe.wait_ge(slot_free[i], freed + j)
                        for a in range(2):
                            last = nc.tensor.matmul(slot[i][:, a * S:(a + 1) * S],
                                                    k_stack[:, p, kc * P:(kc + 1) * P], q_head[:, p % QRING, a, :],
                                                    start=True, stop=True)
                        last.then_inc(slot_ready, 1)
                    if j:
                        values(n, j - 1)
                for i in range(2):
                    pe.wait_ge(slot_free[i], freed + NG * KC)
                values(n, NG * KC - 1)

            def exact_b(n, i, freed):
                for hd in range(NH):
                    g, h = divmod(hd, GH)
                    p, a = divmod(hd, 2)
                    if a == 0:
                        pe.wait_ge(q_masked, 2 * NPAIR * n + 2 * p + 2)
                    for qi in range(ST):
                        k = hd * ST + qi
                        pe.wait_ge(slot_free[0], freed + k)
                        for half in range(2):
                            last = nc.tensor.matmul(slot[0][:, half * S:(half + 1) * S],
                                                    q_head[:, p % QRING, a, qi * P:(qi + 1) * P],
                                                    k_stack[:, p, half * S:(half + 1) * S],
                                                    start=True, stop=True)
                        last.then_inc(slot_ready, 1)
                        pe.wait_ge(exact_probs, NH * ST * i + k + 1)
                        pe.wait_ge(slot_free[1], freed + k)
                        for kc in range(KC):
                            last = nc.tensor.transpose(slot[1][:, kc * P:(kc + 1) * P],
                                                       probs[:, 1, kc * P:(kc + 1) * P], ident[:])
                        last.then_inc(slot_ready, 1)
                    pe.wait_ge(slot_free[1], freed + (hd + 1) * ST)
                    if h == 0:
                        pe.wait_ge(acc_free[g % 2], T_FREE * n + g // 2 + 1)
                    for kc in range(KC):
                        last = nc.tensor.matmul(acc[g % 2][32 * h:32 * h + 32, :], v_aug[:, kc, g % 2, (g // 2) * GH + h, :],
                                                probsT[:, kc, :], start=(kc == 0), stop=(kc == KC - 1))
                    if h == GH - 1:
                        last.then_inc(acc_ready, 1)

            def stage_o(n):
                pe.wait_ge(attn_ready, 2 * n + 2)
                for m in range(ST):
                    if m % 2 == 0:
                        pe.wait_ge(bank_free[m // 2], M_FREE * n + 1)
                    for c in range(CT):
                        last = nc.tensor.matmul(bank[m // 2][:, (m % 2) * D:(m % 2 + 1) * D],
                                                attnT[:, c, m * P:(m + 1) * P], wo[:, c, :],
                                                start=(c == 0), stop=(c == CT - 1))
                    if m % 2:
                        last.then_inc(bank_ready, 1)

            def stage_f(n):
                pe.wait_ge(xn2_ready, n + 1)
                for c in range(CT):
                    pe.wait_ge(bank_free[c], M_FREE * n + 2)
                    for m in range(ST):
                        last = nc.tensor.transpose(bank[c][:, m * P:(m + 1) * P], xn2[:, m, c * P:(c + 1) * P], ident[:])
                    last.then_inc(bank_ready, 1)
                def up(m):
                    if m >= 2:
                        pe.wait_ge(bank_free[m % 2], M_FREE * n + 3 + m // 2)
                    k = 0
                    for c in range(CT):
                        if m == 0:
                            pe.wait_ge(bank_free[c], M_FREE * n + 3)
                        for part in (xh, xl):
                            last = nc.tensor.matmul(bank[m % 2][:], w1_sign[:, c, m * P:(m + 1) * P], part[:, c, :],
                                                    start=(k == 0), stop=(k == 2 * CT - 1))
                            k += 1
                    last.then_inc(bank_ready, 1)

                up(0)
                up(1)
                for a in range(2):
                    pe.wait_ge(acc_free[a], T_FREE * n + 3)
                for m in range(HC):
                    pe.wait_ge(h_split, HC * n + m + 1)
                    for tok in range(ST):
                        for part in (hh, hl):
                            first = m == 0 and tok % 2 == 0 and part is hh
                            done = m == HC - 1 and tok % 2 == 1 and part is hl
                            last = nc.tensor.matmul(acc[tok // 2][:, (tok % 2) * D:(tok % 2 + 1) * D],
                                                    part[:, m % 2, tok * P:(tok + 1) * P], w2_sign[:, m, :],
                                                    start=first, stop=done, skip_group_check=True)
                    if m == HC - 1:
                        last.then_inc(acc_ready, 1)
                    if m + 2 < HC:
                        up(m + 2)

            pe.wait_ge(x0_loaded, 16)
            stage_a(0, 0, first=True)
            stage_v(0, first=True)
            pe.wait_ge(mean_w_set, 1)
            pe.wait_ge(abs_ready, 1)
            for half in range(2):
                for m in range(HC):
                    last = nc.tensor.matmul(bank[half][:, 0:P], mean_w[:],
                                            (y, xn2)[m // ST][:, m % ST, half * P:(half + 1) * P],
                                            start=(m == 0), stop=(m == HC - 1))
                last.then_inc(bank_ready, 1)
            per = A_USES + B_USES
            with pe.Fori(0, NB - 1) as n:
                stage_b(n, per // 2 * n + A_USES // 2)
                stage_a(n + 1, per // 2 * n + per // 2)
                stage_o(n)
                stage_v(per // 2 * n + per // 2)
                stage_f(n)
            stage_b(NB - 1, per // 2 * (NB - 1) + A_USES // 2)
            stage_o(NB - 1)
            stage_f(NB - 1)
            pe.wait_ge(bad_ready, 1)
            nc.tensor.matmul(bank[0][:, 0:1], mean_w[:], bad, start=True, stop=True).then_inc(bad_summed, 1)
            pe.wait_ge(flag_ready, 1)
            with pe.If(pe.value_load(flag[0:1, 0:1]) != 0):
                per_x = A_USES + X_USES
                with pe.Fori(0, NB) as i:
                    stage_a(i + NB, per_x // 2 * i + per // 2 * NB)
                    stage_v(per_x // 2 * i + per // 2 * NB)
                    exact_b(i + NB, i, per_x // 2 * i + (per // 2 * NB + A_USES // 2))
                    stage_o(i + NB)
                    stage_f(i + NB)

        @block.scalar
        def _(act):
            def stage_a(used):
                act.wait_ge(slot_ready, used + 1)
                nc.scalar.copy(xnT[:].rearrange("p c n -> p (c n)"), slot[0][:]).then_inc(slot_free[0], 1)

            def stage_b(used):
                for e in range(B_USES):
                    act.wait_ge(slot_ready, used + e + 1)
                    nc.scalar.activation(probs[:, e % 4, :], slot[e % 2][:], ACT.Exp, scale=SCALE
                                         ).then_inc(slot_free[e % 2], 1)

            def exact_b(i):
                for k in range(NH * ST):
                    act.wait_ge(max_ready, NH * ST * i + k + 1)
                    nc.scalar.activation(probs[:, 1, :], probs[:, 0, :], ACT.Exp, bias=row_max[:, 0:1]
                                         ).then_inc(exact_probs, 1)

            def stage_f(n):
                for c in range(CT):
                    act.wait_ge(bank_ready, M_READY * n + 2 + 3 + c)
                    nc.scalar.copy(xh[:, c, :], bank[c][:]).then_inc(xh_ready, 1)
                for m in range(HC):
                    act.wait_ge(bank_ready, M_READY * n + 2 + 5 + m)
                    if m >= 2:
                        act.wait_ge(h_split, HC * n + m - 1)
                    nc.scalar.activation(hf[:, m % 2, :], bank[m % 2][:], ACT.Gelu, bias=b1_s[:, m:m + 1],
                                         scale=alpha1[:, m:m + 1]).then_inc(bank_free[m % 2], 1)

            act.wait_ge(ffn_loaded, 16 * 7)
            for half, to in enumerate((y, xn2)):
                last = nc.scalar.activation(to[:].rearrange("p m c -> p (m c)"), w2t_raw[:, half, :], ACT.Abs)
            last.then_inc(abs_ready, 1)
            stage_a(0)
            act.wait_ge(signs_ready, 1)
            per = A_USES + B_USES
            with act.Fori(0, NB - 1) as n:
                stage_b(per * n + A_USES)
                stage_a(per * n + per)
                stage_f(n)
            stage_b(per * (NB - 1) + A_USES)
            stage_f(NB - 1)
            act.wait_ge(flag_ready, 1)
            with act.If(act.value_load(flag[0:1, 0:1]) != 0):
                with act.Fori(0, NB) as i:
                    stage_a((A_USES + X_USES) * i + per * NB)
                    exact_b(i)
                    stage_f(i + NB)

        @block.vector
        def _(dve):
            chain = [0, 0]

            def done(ins):
                ins.then_inc(dve_done, 1)
                chain[1] += 1
                return chain[0] + chain[1]

            def counted_loop(times, per_pass, body):
                start = chain[0] + chain[1]
                with dve.Fori(0, times) as i:
                    chain[0], chain[1] = per_pass * i + start, 0
                    body(i)
                    assert chain[1] == per_pass, chain[1]
                chain[0], chain[1] = start + times * per_pass, 0

            def statistics(src, k):
                for m in range(ST):
                    c = done(nc.vector.bn_stats(bn[:, m, :], src[:, m, :]))
                dve.wait_ge(dve_done, c)
                nc.vector.memset(dve_idle, 0.0)
                for m in range(ST):
                    c = done(nc.vector.bn_aggr(mv[:, m, :], bn[:, m, :]))
                dve.wait_ge(dve_done, c)
                nc.vector.tensor_scalar(var[:], mv[:, :, 1], EPS, None, ALU.add).then_inc(var_ready, 1)
                dve.wait_ge(rstd_ready, k)

            def layernorm(dst, src, k, ready):
                statistics(src, k)
                for m in range(ST):
                    last = nc.vector.tensor_scalar(dst[:, m, :], src[:, m, :], mv[:, m, 0:1], rstd[:, m:m + 1],
                                                   ALU.subtract, ALU.mult)
                last.then_inc(ready, 1)

            def norm_x(n, k):
                dve.wait_ge(x_loaded, 16 * n + 16)
                layernorm(xn, xn, k, xn_ready)

            def split(hi, lo, src, bias, signal):
                c = done(nc.vector.tensor_scalar(hi.bitcast(F32R), src, bias, None, ALU.add))
                dve.wait_ge(dve_done, c)
                last = nc.vector.scalar_tensor_tensor(lo.bitcast(F32R), src, bias, hi, ALU.add, ALU.subtract)
                if signal is None:
                    done(last)
                else:
                    last.then_inc(signal, 1)

            def stage_a(used):
                dve.wait_ge(slot_ready, used + 2)
                for t in range(CT):
                    split(q_split[:, 0, t, :], q_split[:, 1, t, :], slot[1][:, t * S:(t + 1) * S], bq_s[:, t:t + 1],
                          slot_free[1] if t == CT - 1 else None)
                for t in range(CT):
                    dve.wait_ge(slot_ready, used + 3 + t)
                    split(k_split[:, 0, t, :], k_split[:, 1, t, :], slot[t][:], bk_s[:, t:t + 1], slot_free[t])

            def stage_v(used):
                for v in range(2):
                    dve.wait_ge(slot_ready, used + 5 + v)
                    for e in range(2):
                        last = nc.vector.tensor_tensor(
                            v_aug[:, v * (KC // 2):(v + 1) * (KC // 2), e, :, 16 * e:16 * e + DH],
                            slot[v][:].rearrange("p (k e h d) -> p k e h d", e=2, h=NH // 2, d=DH)[:, :, e, :, :],
                            bv_s[:].rearrange("p (e h d) -> p e h d", e=2, d=DH)[:, e, :, :].unsqueeze(1)
                            .to_broadcast([P, KC // 2, NH // 2, DH]), ALU.add)
                    last.then_inc(slot_free[v], 1)

            def mask_q(n, p, a):
                if a == 0:
                    dve.wait_ge(stack_ready[p], STACK * n + STACK)
                nc.vector.tensor_scalar(q_head[:, p % QRING, a, :], q_stack[:, p, :], halves[:, a:a + 1], None, ALU.mult
                                        ).then_inc(q_masked, 1)

            def count_mask(n):
                for part in range(2):
                    dve.wait_ge(mask_loaded, 32 * n + 16 * (part + 1))
                    nc.vector.tensor_scalar(stage[:], stage[:], 0.0, None, ALU.not_equal, ALU.add,
                                            accum_out=found[:, n, part:part + 1]).then_inc(mask_used, 1)

            def residual(n):
                dve.wait_ge(res_loaded, 16 * n + 16)
                done(nc.vector.tensor_tensor(y[:], y[:], bo_s[:].unsqueeze(1).to_broadcast([P, ST, D]), ALU.add))

            def take_even(n, t):
                dve.wait_ge(acc_ready, T_READY * n + 2 * t + 1)
                nc.vector.tensor_copy(attn_e, acc[0][:]).then_inc(acc_free[0], 1)
                dve.wait_ge(acc_free[0], T_FREE * n + t + 2)
                done(nc.vector.tensor_scalar(sums[:], attn_e, halves[:, 1:2], None, ALU.mult))
                return done(nc.vector.tensor_scalar(attn_u, attn_e, halves[:, 0:1], None, ALU.mult))

            def take_odd(n, t, even):
                dve.wait_ge(acc_ready, T_READY * n + 2 * t + 2)
                nc.vector.tensor_copy(attn_o, acc[1][:]).then_inc(acc_free[1], 1)
                dve.wait_ge(dve_done, even)
                dve.wait_ge(acc_free[1], T_FREE * n + t + 2)
                c = done(nc.vector.scalar_tensor_tensor(sums[:], attn_o, halves[:, 0:1], sums[:], ALU.mult, ALU.add))
                dve.wait_ge(dve_done, c)
                c = done(nc.vector.reciprocal(rsum, sums[:]))
                dve.wait_ge(dve_done, c)
                c = done(nc.vector.scalar_tensor_tensor(attn_u, attn_o, halves[:, 1:2], attn_u, ALU.mult, ALU.add))
                dve.wait_ge(dve_done, c)
                nc.vector.memset(dve_idle, 0.0)
                c = done(nc.vector.stream_shuffle(attn_o, rsum, list(range(16, 32)) + list(range(16))))
                dve.wait_ge(dve_done, c)
                nc.vector.tensor_tensor(attnT[:, t, :], attn_u, attn_o, ALU.mult).then_inc(attn_ready, 1)

            def check_sums(n, t):
                dve.wait_ge(attn_ready, 2 * n + t + 1)
                for k, (op, bound) in enumerate(((ALU.min, SUM_HI), (ALU.max, SUM_LO))):
                    c = done(nc.vector.scalar_tensor_tensor(attn_o, sums[:], bound, sums[:], op, ALU.is_equal,
                                                            accum_out=found[:, n, 2 + 2 * t + k:3 + 2 * t + k]))
                    dve.wait_ge(dve_done, c)
                return c

            def check_attention(n):
                for t in range(CT):
                    c = done(nc.vector.scalar_tensor_tensor(attn_o, attnT[:, t, :], 0.0, zero[:].to_broadcast([P, S]),
                                                            ALU.mult, ALU.is_equal, accum_out=found[:, n, 6 + t:7 + t]))
                    dve.wait_ge(dve_done, c)

            def stage_o(n, k):
                for a in range(2):
                    dve.wait_ge(bank_ready, M_READY * n + 2 + 1 + a)
                    yy = y[:, 2 * a:2 * a + 2, :].rearrange("p m c -> p (m c)")
                    nc.vector.tensor_tensor(yy, bank[a][:], yy, ALU.add).then_inc(bank_free[a], 1)
                for a in range(2):
                    dve.wait_ge(bank_free[a], M_FREE * n + 2)
                layernorm(xn2, y, k, xn2_ready)
                dve.wait_ge(xn2_ready, n + 1)
                c = done(nc.vector.tensor_tensor(y[:], y[:], b2_s[:].unsqueeze(1).to_broadcast([P, ST, D]), ALU.add))
                return c

            def stage_f(n, y_ready, mask_next):
                for c in range(CT):
                    dve.wait_ge(xh_ready, 2 * n + c + 1)
                    nc.vector.tensor_tensor(xl[:, c, :], bank[c][:], xh[:, c, :].bitcast(F32), ALU.subtract
                                            ).then_inc(bank_free[c], 1)
                for m in range(HC):
                    dve.wait_ge(bank_free[m % 2], M_FREE * n + 4 + m // 2)
                    d = done(nc.vector.tensor_copy(hh[:, m % 2, :], hf[:, m % 2, :]))
                    dve.wait_ge(dve_done, d)
                    nc.vector.tensor_tensor(hl[:, m % 2, :], hf[:, m % 2, :], hh[:, m % 2, :].bitcast(F32), ALU.subtract
                                            ).then_inc(h_split, 1)
                    if mask_next and m >= HC // 2:
                        mask_q(n + 1, (m - HC // 2) // 2, m % 2)
                dve.wait_ge(dve_done, y_ready)
                dve.wait_ge(acc_ready, T_READY * n + 5)
                for a in range(2):
                    to = xn2[:, 2 * a:2 * a + 2, :]
                    nc.vector.tensor_tensor(to, acc[a][:].rearrange("p (m c) -> p m c", c=D),
                                            alpha2[:].unsqueeze(1).to_broadcast([P, 2, D]), ALU.mult
                                            ).then_inc(acc_free[a], 1)
                    dve.wait_ge(acc_free[a], T_FREE * n + 4)
                    nc.vector.tensor_tensor(to, to, y[:, 2 * a:2 * a + 2, :], ALU.add).then_inc(out_ready, 1)

            nc.vector.memset(mean_w[:], 1.0 / HID).then_inc(mean_w_set, 1)
            done(nc.vector.memset(zero[:], 0.0))
            nc.vector.memset(v_aug[:, :, 0, :, 16:32], 1.0).then_inc(acc_free[0], 1)
            nc.vector.memset(v_aug[:, :, 1, :, 0:16], 1.0).then_inc(acc_free[1], 1)
            norm_x(0, 1)
            dve.wait_ge(const_loaded, 48)
            stage_a(0)
            dve.wait_ge(wv_loaded, 32)
            stage_v(0)

            def signs(raw, sign):
                for half in range(2):
                    part = slice(half * T, (half + 1) * T)
                    c = done(nc.vector.tensor_scalar(below, raw[:, part], 0.0, None, ALU.is_lt))
                    dve.wait_ge(dve_done, c)
                    c = done(nc.vector.scalar_tensor_tensor(sign[:, part], raw[:, part], 0.0, below, ALU.is_gt, ALU.subtract))
                    dve.wait_ge(dve_done, c)

            below = attnT[:].rearrange("p c n -> p (c n)")
            dve.wait_ge(ffn_loaded, 16 * 7)
            c = done(nc.vector.tensor_reduce(alpha1[:], w1_raw.rearrange("p a (b d) -> p (a b) d", d=D),
                                             AX.X, ALU.add, apply_absolute_value=True))
            dve.wait_ge(dve_done, c)
            done(nc.vector.tensor_scalar(alpha1[:], alpha1[:], 1.0 / D, None, ALU.mult))
            signs(w2t_raw.rearrange("p a n -> p (a n)"), w2_sign[:].rearrange("p a n -> p (a n)"))
            for p in range(QRING // 2):
                for a in range(2):
                    mask_q(0, p, a)
            signs(stage[:].rearrange("p a n -> p (a n)"), w1_sign[:].rearrange("p a n -> p (a n)"))
            for half in range(2):
                dve.wait_ge(bank_ready, half + 1)
                nc.vector.tensor_copy(alpha2[:, half * P:(half + 1) * P], bank[half][:, 0:P]).then_inc(bank_free[half], 1)
                dve.wait_ge(bank_free[half], 1)
            nc.vector.memset(row_max[:], 0.0).then_inc(signs_ready, 1)

            def mask_pairs(n, first):
                for p in (first, first + 1):
                    for a in range(2):
                        mask_q(n, p, a)

            def fast_batch(n, last):
                mask_pairs(n, 2)
                residual(n)
                count_mask(n)
                if not last:
                    norm_x(n + 1, 2 * n + 2)
                even = take_even(n, 0)
                mask_pairs(n, 4)
                take_odd(n, 0, even)
                mask_pairs(n, 6)
                check_sums(n, 0)
                take_odd(n, 1, take_even(n, 1))
                if not last:
                    stage_a((A_USES + B_USES) * n + (A_USES + B_USES))
                y_ready = stage_o(n, 2 * n + (2 if last else 3))
                if not last:
                    stage_v((A_USES + B_USES) * n + (A_USES + B_USES))
                stage_f(n, y_ready, not last)
                check_sums(n, 1)
                check_attention(n)

            counted_loop(NB - 1, FAST_DONE, lambda n: fast_batch(n, False))
            fast_batch(NB - 1, True)

            mask_found = found[:, :, 0:2]
            good_found = found[:, :, 2:8]
            c = done(nc.vector.tensor_reduce(bad, mask_found, AX.XY, ALU.add))
            c = done(nc.vector.tensor_reduce(bad2, good_found, AX.XY, ALU.add))
            dve.wait_ge(dve_done, c)
            c = done(nc.vector.tensor_scalar(bad2, bad2, -1.0, float(NB * 6 * S), ALU.mult, ALU.add))
            dve.wait_ge(dve_done, c)
            nc.vector.tensor_tensor(bad, bad, bad2, ALU.add).then_inc(bad_ready, 1)
            dve.wait_ge(bad_summed, 1)
            c = done(nc.vector.tensor_scalar(bad_all, bank[0][:, 0:1], 0.0, None, ALU.not_equal))
            dve.wait_ge(dve_done, c)
            nc.vector.tensor_copy(flag[:], bad_all).then_inc(flag_ready, 1)
            dve.wait_ge(flag_ready, 1)

            def exact_batch(i):
                n = i + NB
                norm_x(n, 2 * i + 2 * NB + 1)
                stage_a((A_USES + X_USES) * i + (A_USES + B_USES) * NB)
                stage_v((A_USES + X_USES) * i + (A_USES + B_USES) * NB)
                residual(n)
                dve.wait_ge(mask_loaded, 32 * i + 32 * NB + 32)
                for p in range(NPAIR):
                    dve.wait_ge(stack_ready[p], STACK * n + STACK)
                used = (A_USES + X_USES) * i + ((A_USES + B_USES) * NB + A_USES)
                for hd in range(NH):
                    if hd % 2 == 0:
                        for a in range(2):
                            mask_q(n, hd // 2, a)
                    for qi in range(ST):
                        k = hd * ST + qi
                        dve.wait_ge(slot_ready, used + 2 * k + 1)
                        nc.vector.scalar_tensor_tensor(probs[:, 0, :], slot[0][:], SCALE,
                                                       (stage, probs)[qi // 2][:, qi % 2 + 2 * (qi // 2), :],
                                                       ALU.mult, ALU.add).then_inc(slot_free[0], 1)
                        dve.wait_ge(slot_free[0], (A_USES + X_USES) // 2 * i
                                    + ((A_USES + B_USES) // 2 * NB + A_USES // 2 + k + 1))
                        nc.vector.tensor_reduce(row_max[:], probs[:, 0, :], AX.X, ALU.max, negate=True
                                                ).then_inc(max_ready, 1)
                        dve.wait_ge(slot_ready, used + 2 * k + 2)
                        nc.vector.tensor_copy(probsT[:, :, qi * P:(qi + 1) * P],
                                              slot[1][:].rearrange("p (k q) -> p k q", q=P)).then_inc(slot_free[1], 1)
                    g, h = divmod(hd, GH)
                    if h == GH - 1:
                        if g % 2 == 0:
                            even = take_even(n, g // 2)
                        else:
                            take_odd(n, g // 2, even)
                y_ready = stage_o(n, 2 * i + 2 * NB + 2)
                stage_f(n, y_ready, False)

            with dve.If(dve.value_load(flag[0:1, 0:1]) != 0):
                counted_loop(NB, EXACT_DONE, exact_batch)


FAST_DONE, EXACT_DONE = 49, 43


def _rows(w):
    return np.ascontiguousarray(w.reshape(-1, P, w.shape[1]).transpose(1, 0, 2))


def kernel(**inputs):
    import concourse.bacc as _bacc
    from concourse.bass_utils import run_bass_kernel_spmd as _run

    a = {k: np.asarray(v) for k, v in inputs.items()}
    f = lambda name: a["L0_" + name]
    tile, col, par, ch = np.meshgrid(np.arange(2), np.arange(4), np.arange(2), np.arange(DH), indexing="ij")
    attn_order = (DH * (GH * (2 * tile + par) + col) + ch).reshape(-1)
    par, half, col, ch = np.meshgrid(np.arange(2), np.arange(2), np.arange(4), np.arange(DH), indexing="ij")
    v_order = (DH * (GH * (2 * half + par) + col) + ch).reshape(-1)
    row = lambda v: np.ascontiguousarray(np.broadcast_to(v[None, :], (P, v.shape[0])))
    col_ = lambda v: np.ascontiguousarray(v.reshape(-1, P).T)
    w1, w2 = f("ffn_w1"), f("ffn_w2")
    lane = np.arange(P) % 32 < 16
    arrays = {
        "x": a["x"], "ctx_t": np.ascontiguousarray(a["ctx_1024"].transpose(0, 2, 1)), "mask": a["mask_BxSxS2_ff0"],
        "wq_t": _rows(f("xattn_Wq").T), "wk_t": _rows(f("xattn_Wk").T), "wv_t": _rows(f("xattn_Wv").T[:, v_order]),
        "wo_t": _rows(f("xattn_Wo").T[attn_order]), "bq": col_(f("xattn_bq")), "bk": col_(f("xattn_bk")),
        "bv_row": row(f("xattn_bv")[v_order]), "bo_row": row(f("xattn_bo")),
        "w1": _rows(w1).reshape(P, -1), "w1_t": _rows(w1.T), "w2_t": _rows(w2.T).reshape(P, -1),
        "b1": col_(f("ffn_b1")), "b2_row": row(f("ffn_b2")),
        "ident": np.eye(P, dtype=np.float32), "halves": np.stack([lane, ~lane], 1).astype(np.float32),
    }
    nc = _bacc.Bacc("TRN2", target_bir_lowering=False, num_devices=1)
    args = [nc.dram_tensor("in_" + n, v.shape, F32, kind="ExternalInput").ap() for n, v in arrays.items()]
    out = nc.dram_tensor("out", (NB, S, D), F32, kind="ExternalOutput").ap()
    layer(nc, *args, out)
    r = _run(nc, [{"in_" + n: v for n, v in arrays.items()}], core_ids=[0])
    return r.results[0]["out"]
```

```python
import numpy as np
import concourse.bass as bass
from concourse import mybir
from contextlib import ExitStack

F32 = mybir.dt.float32
F32R = mybir.dt.float32r
I32 = mybir.dt.int32
ALU = mybir.AluOpType
ACT = mybir.ActivationFunctionType
AX = mybir.AxisListType

P = 128
NB, S, T, D = 8, 512, 1024, 256
NH, DH, HID = 16, 16, 1024
CT = D // P
ST = S // P
KC = T // P
HC = HID // P
NG = 4
GH = NH // NG
NPAIR = NH // 2
QRING = 4
SCALE = 0.25
EPS = 1e-5
SUM_LO, SUM_HI = 2.0 ** -30, 2.0 ** 30

A_USES = 6
B_USES = 2 * NG * KC
X_USES = 2 * NH * ST
F_USES = 4
SLOT_A = (2, 3, 1)
SLOT_B = tuple((B_USES - i + 2) // 3 for i in range(3))
SLOT_N = (SLOT_A[0] + SLOT_B[0] + F_USES, SLOT_A[1] + SLOT_B[1], SLOT_A[2] + SLOT_B[2])
SLOT_X = (SLOT_A[0] + X_USES // 2 + F_USES, SLOT_A[1] + X_USES // 2, SLOT_A[2])
M_READY, M_FREE = 12, 4
T_READY, T_FREE = 5, 3
STACK = 8 * 16
FAST_DONE, EXACT_DONE = 45, 39


def layer(nc, x, ctx_t, mask, wq_t, wk_t, wv_t, wo_t, bq, bk, bv_row, bo_row, w1, w1_t, w2_t, b1, b2_row,
          ident_in, halves_in, out):
    es = ExitStack()
    with es:
        def sb(name, shape, dt=F32):
            return es.enter_context(nc.sbuf_tensor(name, shape, dt))

        def sem(name):
            return es.enter_context(nc.semaphore(name))

        ident = sb("ident", [P, P])
        halves = sb("halves", [P, 2])
        zero = sb("zero", [P, 1])
        mean_w = sb("mean_w", [P, P])
        wq, wk, wv, wo = (sb(n, [P, CT, D]) for n in ("wq", "wk", "wv", "wo"))
        w1_sign = sb("w1_sign", [P, CT, HID], F32R)
        w2_sign = sb("w2_sign", [P, HC, D], F32R)
        bq_s, bk_s = sb("bq_s", [P, CT]), sb("bk_s", [P, CT])
        b1_s, alpha1 = sb("b1_s", [P, HC]), sb("alpha1", [P, HC])
        bv_s, bo_s, b2_s, alpha2 = (sb(n, [P, D]) for n in ("bv_s", "bo_s", "b2_s", "alpha2"))
        stage = sb("stage", [P, 2, T])
        ctx_s = sb("ctx_s", [P, CT, T])
        xn = sb("xn", [P, ST, D])
        xnT = sb("xnT", [P, CT, S])
        q_split = sb("q_split", [P, 2, CT, S])
        k_split = sb("k_split", [P, 2, CT, T])
        probsT = k_split[:].rearrange("p a t (b n) -> p (a t b) n", n=S)
        q_stack = sb("q_stack", [P, NPAIR, S])
        q_head = sb("q_head", [P, QRING, 2, S], F32R)
        k_stack = sb("k_stack", [P, NPAIR, T], F32R)
        v_aug = sb("v_aug", [P, KC, 2, NH // 2, 32])
        probs = sb("probs", [P, 4, T])
        w2t_raw = probs[:, 0:2, :]
        sums = sb("sums", [P, S])
        attnT = sb("attnT", [P, CT, S])
        y = sb("y", [P, ST, D])
        xn2 = sb("xn2", [P, ST, D])
        xh, xl = sb("xh", [P, CT, S], F32R), sb("xl", [P, CT, S], F32R)
        hf = sb("hf", [P, 2, S])
        attn_e, attn_o = hf[:, 0, :], hf[:, 1, :]
        xn2_halves = xn2[:].rearrange("p (a m) c -> p a (m c)", a=2)
        rsum, attn_u = xn2_halves[:, 0, :], xn2_halves[:, 1, :]
        hh, hl = sb("hh", [P, 2, S], F32R), sb("hl", [P, 2, S], F32R)
        bn, mv = sb("bn", [P, ST, 6]), sb("mv", [P, ST, 2])
        var, rstd, minus_half = sb("var", [P, ST]), sb("rstd", [P, ST]), sb("minus_half", [P, ST])
        row_max = sb("row_max", [P, 1])
        found = sb("found", [P, NB, 8])
        small = sb("small", [P, 5])
        bad, bad2, bad_all, dve_idle, pool_idle = (small[:, k:k + 1] for k in range(5))
        flag = sb("flag", [P, 1], I32)

        slot = [es.enter_context(nc.psum_tensor(f"slot{i}", [P, 2 * S], F32)) for i in range(3)]
        acc = [es.enter_context(nc.psum_tensor(f"acc{i}", [P, S], F32)) for i in range(2)]
        bank = [slot[2][:, a * S:(a + 1) * S] for a in range(2)]

        def chunk_bank(m):
            return slot[0][:, m % 2 * S:(m % 2 + 1) * S] if m % 4 < 2 else bank[m % 2]

        def chunk_free(m):
            return slot_free[0] if m % 4 < 2 else bank_free[m % 2]

        def chunks_taken(m, n, f0):
            return f0 + 2 * (m // 4) + m % 2 + 1 if m % 4 < 2 else M_FREE * n + 4 + m // 4

        x0_loaded, last_stored = sem("x0_loaded"), sem("last_stored")
        ident_loaded, wk_loaded = sem("ident_loaded"), sem("wk_loaded")
        wq_loaded, wv_loaded, ctx0_loaded = sem("wq_loaded"), sem("wv_loaded"), [sem("ctx0_loaded0"), sem("ctx0_loaded1")]
        const_loaded, w2_loaded, ffn_loaded = sem("const_loaded"), sem("w2_loaded"), sem("ffn_loaded")
        x_loaded, ctx_loaded, res_loaded = sem("x_loaded"), sem("ctx_loaded"), sem("res_loaded")
        mask_loaded, mask_used = sem("mask_loaded"), sem("mask_used")
        mean_w_set, exponent_set, abs_ready = sem("mean_w_set"), sem("exponent_set"), sem("abs_ready")
        w2_used, signs_ready = sem("w2_used"), sem("signs_ready")
        var_ready, rstd_ready = sem("var_ready"), sem("rstd_ready")
        xn_ready, xn2_ready = sem("xn_ready"), sem("xn2_ready")
        stack_ready = [sem(f"stack_ready{g}") for g in range(NG)]
        slot_ready, slot_free = sem("slot_ready"), [sem(f"slot{i}_free") for i in range(3)]
        acc_ready, acc_free = sem("acc_ready"), [sem("acc0_free"), sem("acc1_free")]
        bank_ready, bank_free = sem("bank_ready"), [sem("bank0_free"), sem("bank1_free")]
        hi_ready, h_used = sem("hi_ready"), sem("h_used")
        attn_ready, h_split, out_ready, out_stored = sem("attn_ready"), sem("h_split"), sem("out_ready"), sem("out_stored")
        pool_ticks = sem("pool_ticks")
        q_masked, xh_ready = sem("q_masked"), sem("xh_ready")
        max_ready, exact_probs = sem("max_ready"), sem("exact_probs")
        dve_done, bad_ready, bad_summed, flag_ready = sem("dve_done"), sem("bad_ready"), sem("bad_summed"), sem("flag_ready")

        def used_before_b(n):
            return [SLOT_N[k] * n + SLOT_A[k] for k in range(3)]

        def used_after_b(n):
            return [SLOT_N[k] * n + (SLOT_A[k] + SLOT_B[k]) for k in range(3)]

        def used_exact(i):
            return [SLOT_X[k] * i + SLOT_N[k] * NB for k in range(3)]

        def used_before_f(n, last=False):
            return SLOT_N[0] * n + (SLOT_A[0] + SLOT_B[0] + (0 if last else SLOT_A[0]))

        block = es.enter_context(nc.Block())

        @block.sync
        def _(sp):
            sp.dma_start(xn[:], x[0].rearrange("(m p) c -> p m c", p=P)).then_inc(x0_loaded, 16)
            sp.dma_start(wk[:], wk_t).then_inc(wk_loaded, 16)
            for half in range(2):
                sp.dma_start(ctx_s[:, :, half * S:(half + 1) * S],
                             ctx_t[0].rearrange("(t p) n -> p t n", p=P)[:, :, half * S:(half + 1) * S]
                             ).then_inc(ctx0_loaded[half], 16)
            sp.dma_start(ident[:], ident_in).then_inc(ident_loaded, 16)
            sp.dma_start(wq[:], wq_t).then_inc(wq_loaded, 16)
            sp.dma_start(bk_s[:], bk).then_inc(const_loaded, 16)
            sp.dma_start(bq_s[:], bq).then_inc(const_loaded, 16)
            sp.dma_start(halves[:], halves_in).then_inc(const_loaded, 16)
            sp.dma_start(wv[:], wv_t).then_inc(wv_loaded, 16)
            sp.dma_start(bv_s[:], bv_row).then_inc(wv_loaded, 16)
            sp.wait_ge(ctx0_loaded[1], 16)
            sp.dma_start(w2t_raw.rearrange("p a n -> p (a n)"), w2_t).then_inc(w2_loaded, 16)
            sp.dma_start(stage[:], w1_t).then_inc(ffn_loaded, 16)
            for m, to in enumerate((hf, attnT)):
                sp.dma_start(to[:].rearrange("p c n -> p (c n)"), w1[:, m * T:(m + 1) * T]).then_inc(ffn_loaded, 16)
            sp.dma_start(b1_s[:], b1).then_inc(ffn_loaded, 16)
            sp.dma_start(wo[:], wo_t).then_inc(ffn_loaded, 16)
            sp.dma_start(bo_s[:], bo_row).then_inc(ffn_loaded, 16)
            sp.dma_start(b2_s[:], b2_row).then_inc(ffn_loaded, 16)

            def build_stacks(used):
                sp.wait_ge(slot_free[2], used[2] + 1)
                sp.wait_ge(slot_free[0], used[0] + 1)
                sp.wait_ge(slot_free[1], used[1] + 2)
                for g in range(NG):
                    of = slice(2 * DH * g, 2 * DH * (g + 1))
                    for r in range(4):
                        to = slice(2 * DH * r, 2 * DH * (r + 1))
                        sp.dma_start(q_stack[to, 2 * g:2 * g + 2, :], q_split[of, r // 2, :, :]
                                     ).then_inc(stack_ready[g], 16)
                        sp.dma_start(k_stack[to, 2 * g:2 * g + 2, :].bitcast(F32), k_split[of, r % 2, :, :]
                                     ).then_inc(stack_ready[g], 16)

            build_stacks((0, 0, 0))
            with sp.Fori(0, NB - 1) as n:
                build_stacks(used_after_b(n))
            for a in range(2):
                sp.wait_ge(out_ready, 2 * NB - 1 + a)
                sp.dma_start(out[NB - 1, 2 * P * a:2 * P * (a + 1), :].rearrange("(m p) c -> p m c", p=P),
                             xn2[:, 2 * a:2 * a + 2, :]).then_inc(last_stored, 16)
            sp.wait_ge(last_stored, 32)
            sp.wait_ge(flag_ready, 1)
            with sp.If(sp.value_load(flag[0:1, 0:1]) != 0):
                with sp.Fori(0, NB) as i:
                    build_stacks(used_exact(i))

        @block.gpsimd
        def _(pool):
            nc.gpsimd.memset(minus_half[:], -0.5).then_inc(exponent_set, 1)
            pool.wait_ge(exponent_set, 1)

            def hold(semaphore, value, ticks):
                if not (isinstance(ticks, int) and ticks == 0):
                    pool.wait_ge(pool_ticks, ticks)
                pool.wait_ge(semaphore, value)
                nc.gpsimd.tensor_tensor(pool_idle, minus_half[:, 0:1], minus_half[:, 0:1], ALU.mult
                                        ).then_inc(pool_ticks, 1)

            def power(k):
                pool.wait_ge(var_ready, k)
                nc.gpsimd.tensor_tensor(rstd[:], var[:], minus_half[:], ALU.pow).then_inc(rstd_ready, 1)

            def store(b, n, ticks, stored):
                hold(out_ready, 2 * n + 2, ticks)
                pool.dma_start(out[b].rearrange("(m p) c -> p m c", p=P), xn2[:]).then_inc(out_stored, 16)
                hold(out_stored, stored + 16, ticks + 1)

            def mask_part(b, n, part):
                pool.dma_start(stage[:],
                               mask[b, part * 2 * P:(part + 1) * 2 * P, :].rearrange("(m p) k -> p m k", p=P)
                               ).then_inc(mask_loaded, 16)

            def batch(n, last):
                pool.dma_start(y[:], x[n].rearrange("(m p) c -> p m c", p=P)).then_inc(res_loaded, 16)
                if not last:
                    hold(slot_ready, (A_USES + B_USES) * n + A_USES, 4 * n + 1)
                    pool.dma_start(xn[:], x[n + 1].rearrange("(m p) c -> p m c", p=P)).then_inc(x_loaded, 16)
                    pool.dma_start(ctx_s[:], ctx_t[n + 1].rearrange("(t p) n -> p t n", p=P)).then_inc(ctx_loaded, 16)
                mask_part(n, n, 0)
                hold(mask_used, 2 * n + 1, 4 * n + (1 if last else 2))
                mask_part(n, n, 1)
                if not last:
                    power(2 * n + 2)
                    power(2 * n + 3)
                    store(n, n, 4 * n + 3, 16 * n)
                else:
                    power(2 * n + 2)
                    pool.wait_ge(last_stored, 32)

            hold(exponent_set, 1, 0)
            power(1)
            pool.wait_ge(signs_ready, 1)
            with pool.Fori(0, NB - 1) as n:
                batch(n, False)
            batch(NB - 1, True)
            pool.wait_ge(flag_ready, 1)
            with pool.If(pool.value_load(flag[0:1, 0:1]) != 0):
                with pool.Fori(0, NB) as i:
                    pool.dma_start(xn[:], x[i].rearrange("(m p) c -> p m c", p=P)).then_inc(x_loaded, 16)
                    pool.dma_start(ctx_s[:], ctx_t[i].rearrange("(t p) n -> p t n", p=P)).then_inc(ctx_loaded, 16)
                    pool.dma_start(y[:], x[i].rearrange("(m p) c -> p m c", p=P)).then_inc(res_loaded, 16)
                    for half, to in enumerate((stage[:], probs[:, 2:4, :])):
                        pool.dma_start(to, mask[i, 2 * half * P:2 * (half + 1) * P, :].rearrange("(m p) k -> p m k", p=P)
                                       ).then_inc(mask_loaded, 16)
                    power(2 * i + 2 * NB + 1)
                    power(2 * i + 2 * NB + 2)
                    store(i, i + NB, 2 * i + (4 * NB - 2), 16 * i + 16 * (NB - 1))

        @block.tensor
        def _(pe):
            def transpose_x(n, used):
                pe.wait_ge(xn_ready, n + 1)
                if used is not None:
                    pe.wait_ge(slot_free[1], used[1])
                for c in range(CT):
                    for m in range(ST):
                        last = nc.tensor.transpose(slot[1][:, c * S + m * P:c * S + (m + 1) * P],
                                                   xn[:, m, c * P:(c + 1) * P], ident[:])
                last.then_inc(slot_ready, 1)

            def project_k(t, to, first=False):
                for half in range(2):
                    if first:
                        pe.wait_ge(ctx0_loaded[half], 16)
                    for c in range(CT):
                        last = nc.tensor.matmul(slot[to][:, half * S:(half + 1) * S], wk[:, c, t * P:(t + 1) * P],
                                                ctx_s[:, c, half * S:(half + 1) * S],
                                                start=(c == 0), stop=(c == CT - 1))
                last.then_inc(slot_ready, 1)

            def project_q(slot1_used):
                pe.wait_ge(slot_free[1], slot1_used + 1)
                for t in range(CT):
                    for c in range(CT):
                        last = nc.tensor.matmul(slot[0][:, t * S:(t + 1) * S], wq[:, c, t * P:(t + 1) * P],
                                                xnT[:, c, :], start=(c == 0), stop=(c == CT - 1))
                last.then_inc(slot_ready, 1)

            def stage_a(n, used):
                pe.wait_ge(slot_free[2], used[2])
                pe.wait_ge(ctx_loaded, 16 * n)
                project_k(0, 2)
                pe.wait_ge(slot_free[0], used[0])
                project_q(used[1])
                project_k(1, 1)

            def project_v(chunks, used):
                for kc in chunks:
                    v, kk = divmod(kc, KC // 2)
                    if kk == 0:
                        pe.wait_ge(slot_free[v], used[v] + 1 + v)
                    for c in range(CT):
                        last = nc.tensor.matmul(slot[v][:, kk * D:(kk + 1) * D], ctx_s[:, c, kc * P:(kc + 1) * P],
                                                wv[:, c, :], start=(c == 0), stop=(c == CT - 1))
                    if kk == KC // 2 - 1:
                        last.then_inc(slot_ready, 1)

            def scores(n, e):
                j, i = divmod(e, 2)
                g, kc = divmod(j, KC)
                p = 2 * g + i
                if kc == 0:
                    pe.wait_ge(q_masked, 2 * NPAIR * n + 2 * p + 2)
                if e == 2:
                    for a in range(2):
                        pe.wait_ge(bank_free[a], M_FREE * n + 1)
                pe.wait_ge(slot_free[e % 3], used_before_b(n)[e % 3] + e // 3)
                for a in range(2):
                    last = nc.tensor.matmul(slot[e % 3][:, a * S:(a + 1) * S],
                                            k_stack[:, p, kc * P:(kc + 1) * P], q_head[:, p % QRING, a, :],
                                            start=True, stop=True)
                last.then_inc(slot_ready, 1)

            def values(n, j):
                g, kc = divmod(j, KC)
                if kc == 0:
                    pe.wait_ge(acc_free[g % 2], T_FREE * n + g // 2 + 1)
                e = 2 * j + 1
                pe.wait_ge(slot_free[e % 3], used_before_b(n)[e % 3] + e // 3 + 1)
                for h in range(GH):
                    e = 2 * j + h // 2
                    last = nc.tensor.matmul(acc[g % 2][32 * h:32 * h + 32, :], v_aug[:, kc, g % 2, (g // 2) * GH + h, :],
                                            probs[:, e % 4, (h % 2) * S:(h % 2 + 1) * S],
                                            start=(kc == 0), stop=(kc == KC - 1))
                if kc == KC - 1:
                    last.then_inc(acc_ready, 1)

            def stage_b(n, last):
                for j in range(1, NG * KC):
                    scores(n, 2 * j)
                    scores(n, 2 * j + 1)
                    values(n, j - 1)
                if not last:
                    transpose_x(n + 1, used_after_b(n))
                values(n, NG * KC - 1)

            def exact_b(n, i, used):
                for hd in range(NH):
                    g, h = divmod(hd, GH)
                    p, a = divmod(hd, 2)
                    if a == 0:
                        pe.wait_ge(q_masked, 2 * NPAIR * n + 2 * p + 2)
                    for qi in range(ST):
                        k = hd * ST + qi
                        pe.wait_ge(slot_free[0], used[0] + SLOT_A[0] + k)
                        for half in range(2):
                            last = nc.tensor.matmul(slot[0][:, half * S:(half + 1) * S],
                                                    q_head[:, p % QRING, a, qi * P:(qi + 1) * P],
                                                    k_stack[:, p, half * S:(half + 1) * S],
                                                    start=True, stop=True)
                        last.then_inc(slot_ready, 1)
                        pe.wait_ge(exact_probs, NH * ST * i + k + 1)
                        pe.wait_ge(slot_free[1], used[1] + SLOT_A[1] + k)
                        for kc in range(KC):
                            last = nc.tensor.transpose(slot[1][:, kc * P:(kc + 1) * P],
                                                       probs[:, 1, kc * P:(kc + 1) * P], ident[:])
                        last.then_inc(slot_ready, 1)
                    pe.wait_ge(slot_free[1], used[1] + SLOT_A[1] + (hd + 1) * ST)
                    if h == 0:
                        pe.wait_ge(acc_free[g % 2], T_FREE * n + g // 2 + 1)
                    for kc in range(KC):
                        last = nc.tensor.matmul(acc[g % 2][32 * h:32 * h + 32, :], v_aug[:, kc, g % 2, (g // 2) * GH + h, :],
                                                probsT[:, kc, :], start=(kc == 0), stop=(kc == KC - 1))
                    if h == GH - 1:
                        last.then_inc(acc_ready, 1)

            def stage_o(n, slot2_used):
                pe.wait_ge(slot_free[2], slot2_used)
                for c in range(CT):
                    if c == 0:
                        pe.wait_ge(attn_ready, 4 * n + 2)
                    for m in range(ST):
                        if m % 2 == 0:
                            if c == 0:
                                pe.wait_ge(bank_free[m // 2], M_FREE * n + 1)
                            else:
                                pe.wait_ge(attn_ready, 4 * n + 3 + m // 2)
                        last = nc.tensor.matmul(bank[m // 2][:, (m % 2) * D:(m % 2 + 1) * D],
                                                attnT[:, c, m * P:(m + 1) * P], wo[:, c, :],
                                                start=(c == 0 and m % 2 == 0), stop=(c == CT - 1 and m % 2 == 1),
                                                skip_group_check=True)
                        if c == CT - 1 and m % 2:
                            last.then_inc(bank_ready, 1)

            def transpose_y(n):
                pe.wait_ge(xn2_ready, n + 1)
                for c in range(CT):
                    pe.wait_ge(bank_free[c], M_FREE * n + 2)
                    for m in range(ST):
                        last = nc.tensor.transpose(bank[c][:, m * P:(m + 1) * P], xn2[:, m, c * P:(c + 1) * P], ident[:])
                    last.then_inc(bank_ready, 1)

            def up(n, m, f0):
                if m >= 4:
                    pe.wait_ge(chunk_free(m), chunks_taken(m - 4, n, f0))
                elif m == 0:
                    pe.wait_ge(slot_free[0], f0)
                k = 0
                for c in range(CT):
                    if m == 0:
                        pe.wait_ge(bank_free[c], M_FREE * n + 3)
                    for part in (xh, xl):
                        last = nc.tensor.matmul(chunk_bank(m), w1_sign[:, c, m * P:(m + 1) * P], part[:, c, :],
                                                start=(k == 0), stop=(k == 2 * CT - 1))
                        k += 1
                last.then_inc(bank_ready, 1)

            def down(n, m):
                pe.wait_ge(h_split, HC * n + m + 1)
                for tok in range(ST):
                    for part in (hh, hl):
                        first = m == 0 and tok % 2 == 0 and part is hh
                        done = m == HC - 1 and tok % 2 == 1 and part is hl
                        last = nc.tensor.matmul(acc[tok // 2][:, (tok % 2) * D:(tok % 2 + 1) * D],
                                                part[:, m % 2, tok * P:(tok + 1) * P], w2_sign[:, m, :],
                                                start=first, stop=done, skip_group_check=True)
                last.then_inc(acc_ready if m == HC - 1 else h_used, 1)

            def stage_f(n, f0, scores_next):
                for m in range(4):
                    up(n, m, f0)
                for a in range(2):
                    pe.wait_ge(acc_free[a], T_FREE * n + 3)
                for m in range(HC):
                    if m >= HC - 2 and scores_next:
                        scores(n + 1, m - (HC - 2))
                    down(n, m)
                    if m + 4 < HC:
                        up(n, m + 4, f0)

            pe.wait_ge(wk_loaded, 16)
            project_k(0, 2, first=True)
            pe.wait_ge(ident_loaded, 16)
            transpose_x(0, None)
            pe.wait_ge(wq_loaded, 16)
            project_q(0)
            project_k(1, 1)
            pe.wait_ge(wv_loaded, 32)
            project_v(range(KC), (0, 0))
            pe.wait_ge(mean_w_set, 1)
            pe.wait_ge(abs_ready, 1)
            pe.wait_ge(slot_free[2], 1)
            for half in range(2):
                for m in range(HC):
                    last = nc.tensor.matmul(bank[half][:, 0:P], mean_w[:],
                                            (y, xn2)[m // ST][:, m % ST, half * P:(half + 1) * P],
                                            start=(m == 0), stop=(m == HC - 1))
                last.then_inc(bank_ready, 1)
            scores(0, 0)
            scores(0, 1)
            with pe.Fori(0, NB - 1) as n:
                used = used_after_b(n)
                stage_b(n, False)
                stage_a(n + 1, used)
                stage_o(n, used[2] + 1)
                project_v(range(KC - 1), used)
                transpose_y(n)
                project_v(range(KC - 1, KC), used)
                stage_f(n, used_before_f(n), True)
            stage_b(NB - 1, True)
            stage_o(NB - 1, used_after_b(NB - 1)[2])
            transpose_y(NB - 1)
            stage_f(NB - 1, used_before_f(NB - 1, last=True), False)
            pe.wait_ge(bad_ready, 1)
            nc.tensor.matmul(bank[0][:, 0:1], mean_w[:], bad, start=True, stop=True).then_inc(bad_summed, 1)
            pe.wait_ge(flag_ready, 1)
            with pe.If(pe.value_load(flag[0:1, 0:1]) != 0):
                with pe.Fori(0, NB) as i:
                    used = used_exact(i)
                    for a in range(2):
                        pe.wait_ge(bank_free[a], M_FREE * i + (M_FREE * NB + 1))
                    transpose_x(i + NB, used)
                    stage_a(i + NB, used)
                    project_v(range(KC), used)
                    exact_b(i + NB, i, used)
                    stage_o(i + NB, used[2] + 1)
                    transpose_y(i + NB)
                    stage_f(i + NB, SLOT_X[0] * i + (SLOT_N[0] * NB + SLOT_A[0] + X_USES // 2), False)

        @block.scalar
        def _(act):
            def stage_a(used):
                act.wait_ge(slot_ready, used + 2)
                nc.scalar.activation(k_split[:, 0, 0, :].bitcast(F32R), slot[2][:], ACT.Identity, bias=bk_s[:, 0:1]
                                     ).then_inc(hi_ready, 1)
                act.wait_ge(slot_ready, used + 3)
                for t in range(CT):
                    nc.scalar.activation(q_split[:, 0, t, :].bitcast(F32R), slot[0][:, t * S:(t + 1) * S], ACT.Identity,
                                         bias=bq_s[:, t:t + 1]).then_inc(hi_ready, 1)
                act.wait_ge(slot_ready, used + 4)
                nc.scalar.activation(k_split[:, 0, 1, :].bitcast(F32R), slot[1][:], ACT.Identity, bias=bk_s[:, 1:2]
                                     ).then_inc(hi_ready, 1)

            def stage_b(used):
                for e in range(B_USES):
                    act.wait_ge(slot_ready, used + e + 1)
                    nc.scalar.activation(probs[:, e % 4, :], slot[e % 3][:], ACT.Exp, scale=SCALE
                                         ).then_inc(slot_free[e % 3], 1)

            def exact_b(i):
                for k in range(NH * ST):
                    act.wait_ge(max_ready, NH * ST * i + k + 1)
                    nc.scalar.activation(probs[:, 1, :], probs[:, 0, :], ACT.Exp, bias=row_max[:, 0:1]
                                         ).then_inc(exact_probs, 1)

            def stage_f(n):
                for c in range(CT):
                    act.wait_ge(bank_ready, M_READY * n + 2 + 3 + c)
                    nc.scalar.copy(xh[:, c, :], bank[c]).then_inc(xh_ready, 1)
                for m in range(HC):
                    act.wait_ge(bank_ready, M_READY * n + 2 + 5 + m)
                    if m >= 2:
                        act.wait_ge(h_split, HC * n + m - 1)
                    nc.scalar.activation(hf[:, m % 2, :], chunk_bank(m), ACT.Gelu, bias=b1_s[:, m:m + 1],
                                         scale=alpha1[:, m:m + 1]).then_inc(chunk_free(m), 1)

            act.wait_ge(const_loaded, 48)
            stage_a(0)
            act.wait_ge(w2_loaded, 16)
            for half, to in enumerate((y, xn2)):
                last = nc.scalar.activation(to[:].rearrange("p m c -> p (m c)"), w2t_raw[:, half, :], ACT.Abs)
            last.then_inc(abs_ready, 1)
            act.wait_ge(w2_used, 1)
            per = A_USES + B_USES
            with act.Fori(0, NB - 1) as n:
                stage_b(per * n + A_USES)
                stage_a(per * n + per)
                stage_f(n)
            stage_b(per * (NB - 1) + A_USES)
            stage_f(NB - 1)
            act.wait_ge(flag_ready, 1)
            with act.If(act.value_load(flag[0:1, 0:1]) != 0):
                with act.Fori(0, NB) as i:
                    stage_a((A_USES + X_USES) * i + per * NB)
                    exact_b(i)
                    stage_f(i + NB)

        @block.vector
        def _(dve):
            chain = [0, 0]

            def done(ins):
                ins.then_inc(dve_done, 1)
                chain[1] += 1
                return chain[0] + chain[1]

            def counted_loop(times, per_pass, body):
                start = chain[0] + chain[1]
                with dve.Fori(0, times) as i:
                    chain[0], chain[1] = per_pass * i + start, 0
                    body(i)
                    assert chain[1] == per_pass, chain[1]
                chain[0], chain[1] = start + times * per_pass, 0

            def statistics(src, k):
                for m in range(ST):
                    c = done(nc.vector.bn_stats(bn[:, m, :], src[:, m, :]))
                dve.wait_ge(dve_done, c)
                nc.vector.memset(dve_idle, 0.0)
                for m in range(ST):
                    c = done(nc.vector.bn_aggr(mv[:, m, :], bn[:, m, :]))
                dve.wait_ge(dve_done, c)
                nc.vector.tensor_scalar(var[:], mv[:, :, 1], EPS, None, ALU.add).then_inc(var_ready, 1)
                dve.wait_ge(rstd_ready, k)

            def layernorm(dst, src, k, ready):
                statistics(src, k)
                for m in range(ST):
                    last = nc.vector.tensor_scalar(dst[:, m, :], src[:, m, :], mv[:, m, 0:1], rstd[:, m:m + 1],
                                                   ALU.subtract, ALU.mult)
                last.then_inc(ready, 1)

            def norm_x(n, k):
                if isinstance(n, int) and n == 0:
                    dve.wait_ge(x0_loaded, 16)
                else:
                    dve.wait_ge(x_loaded, 16 * n)
                layernorm(xn, xn, k, xn_ready)

            def copy_x(used, first=False):
                dve.wait_ge(slot_ready, used + (2 if first else 1))
                nc.vector.tensor_copy(xnT[:].rearrange("p c n -> p (c n)"), slot[1][:]).then_inc(slot_free[1], 1)

            def lo(split, t, src, bias, signal):
                last = nc.vector.scalar_tensor_tensor(split[:, 1, t, :].bitcast(F32R), src, bias[:, t:t + 1],
                                                      split[:, 0, t, :], ALU.add, ALU.subtract)
                if signal is None:
                    done(last)
                else:
                    last.then_inc(signal, 1)

            def lo_k(n, t):
                dve.wait_ge(hi_ready, 4 * n + 1 + 3 * t)
                lo(k_split, t, slot[2 - t][:], bk_s, slot_free[2 - t])

            def lo_q(n):
                for t in range(CT):
                    dve.wait_ge(hi_ready, 4 * n + 2 + t)
                    lo(q_split, t, slot[0][:, t * S:(t + 1) * S], bq_s, slot_free[0] if t == CT - 1 else None)

            def stage_a(n):
                lo_k(n, 0)
                lo_q(n)
                lo_k(n, 1)

            def take_v(used, v):
                dve.wait_ge(slot_ready, used + 5 + v)
                for e in range(2):
                    last = nc.vector.tensor_tensor(
                        v_aug[:, v * (KC // 2):(v + 1) * (KC // 2), e, :, 16 * e:16 * e + DH],
                        slot[v][:].rearrange("p (k e h d) -> p k e h d", e=2, h=NH // 2, d=DH)[:, :, e, :, :],
                        bv_s[:].rearrange("p (e h d) -> p e h d", e=2, d=DH)[:, e, :, :].unsqueeze(1)
                        .to_broadcast([P, KC // 2, NH // 2, DH]), ALU.add)
                last.then_inc(slot_free[v], 1)

            def mask_q(n, p, a):
                if a == 0 and p % 2 == 0:
                    dve.wait_ge(stack_ready[p // 2], STACK * n + STACK)
                nc.vector.tensor_scalar(q_head[:, p % QRING, a, :], q_stack[:, p, :], halves[:, a:a + 1], None, ALU.mult
                                        ).then_inc(q_masked, 1)

            def mask_pairs(n, first):
                for p in (first, first + 1):
                    for a in range(2):
                        mask_q(n, p, a)

            def count_mask(n, part):
                dve.wait_ge(mask_loaded, 32 * n + 16 * (part + 1))
                nc.vector.tensor_scalar(stage[:], stage[:], 0.0, None, ALU.not_equal, ALU.add,
                                        accum_out=found[:, n, part:part + 1]).then_inc(mask_used, 1)

            def residual(n):
                dve.wait_ge(res_loaded, 16 * n + 16)
                done(nc.vector.tensor_tensor(y[:], y[:], bo_s[:].unsqueeze(1).to_broadcast([P, ST, D]), ALU.add))

            def take_even(n, t):
                dve.wait_ge(acc_ready, T_READY * n + 2 * t + 1)
                nc.vector.tensor_copy(attn_e, acc[0][:]).then_inc(acc_free[0], 1)
                dve.wait_ge(acc_free[0], T_FREE * n + t + 2)
                done(nc.vector.tensor_scalar(sums[:], attn_e, halves[:, 1:2], None, ALU.mult))
                return done(nc.vector.tensor_scalar(attn_u, attn_e, halves[:, 0:1], None, ALU.mult))

            def take_odd(n, t, even, parts=1):
                dve.wait_ge(acc_ready, T_READY * n + 2 * t + 2)
                nc.vector.tensor_copy(attn_o, acc[1][:]).then_inc(acc_free[1], 1)
                dve.wait_ge(dve_done, even)
                dve.wait_ge(acc_free[1], T_FREE * n + t + 2)
                for part in range(parts):
                    at = slice(part * S // parts, (part + 1) * S // parts)
                    c = done(nc.vector.scalar_tensor_tensor(sums[:, at], attn_o[:, at], halves[:, 0:1], sums[:, at],
                                                            ALU.mult, ALU.add))
                    dve.wait_ge(dve_done, c)
                    c = done(nc.vector.reciprocal(rsum[:, at], sums[:, at]))
                    dve.wait_ge(dve_done, c)
                    c = done(nc.vector.scalar_tensor_tensor(attn_u[:, at], attn_o[:, at], halves[:, 1:2], attn_u[:, at],
                                                            ALU.mult, ALU.add))
                    dve.wait_ge(dve_done, c)
                    nc.vector.memset(dve_idle, 0.0)
                    c = done(nc.vector.stream_shuffle(attn_o[:, at], rsum[:, at], list(range(16, 32)) + list(range(16))))
                    dve.wait_ge(dve_done, c)
                    nc.vector.tensor_tensor(attnT[:, t, at], attn_u[:, at], attn_o[:, at], ALU.mult
                                            ).then_inc(attn_ready, 2 // parts)

            def check_sums(n, t):
                dve.wait_ge(attn_ready, 4 * n + 2 * t + 2)
                for k, (op, bound) in enumerate(((ALU.min, SUM_HI), (ALU.max, SUM_LO))):
                    c = done(nc.vector.scalar_tensor_tensor(attn_o, sums[:], bound, sums[:], op, ALU.is_equal,
                                                            accum_out=found[:, n, 2 + 2 * t + k:3 + 2 * t + k]))
                    dve.wait_ge(dve_done, c)
                return c

            def check_attention(n):
                for t in range(CT):
                    c = done(nc.vector.scalar_tensor_tensor(attn_o, attnT[:, t, :], 0.0, zero[:].to_broadcast([P, S]),
                                                            ALU.mult, ALU.is_equal, accum_out=found[:, n, 6 + t:7 + t]))
                    dve.wait_ge(dve_done, c)

            def stage_o(n, k):
                for a in range(2):
                    dve.wait_ge(bank_ready, M_READY * n + 2 + 1 + a)
                    yy = y[:, 2 * a:2 * a + 2, :].rearrange("p m c -> p (m c)")
                    nc.vector.tensor_tensor(yy, bank[a], yy, ALU.add).then_inc(bank_free[a], 1)
                for a in range(2):
                    dve.wait_ge(bank_free[a], M_FREE * n + 2)
                layernorm(xn2, y, k, xn2_ready)

            def add_b2(n):
                dve.wait_ge(xn2_ready, n + 1)
                return done(nc.vector.tensor_tensor(y[:], y[:], b2_s[:].unsqueeze(1).to_broadcast([P, ST, D]), ALU.add))

            def stage_f(n, f0, used_next):
                v_next = used_next is not None
                if v_next:
                    take_v(used_next, 0)
                for c in range(CT):
                    dve.wait_ge(xh_ready, 2 * n + c + 1)
                    nc.vector.tensor_tensor(xl[:, c, :], bank[c], xh[:, c, :].bitcast(F32), ALU.subtract
                                            ).then_inc(bank_free[c], 1)
                if v_next:
                    take_v(used_next, 1)
                for m in range(HC):
                    if m == 2 and not v_next:
                        y_ready = add_b2(n)
                    dve.wait_ge(chunk_free(m), chunks_taken(m, n, f0))
                    if m >= 2:
                        dve.wait_ge(h_used, (HC - 1) * n + m - 1)
                    d = done(nc.vector.tensor_copy(hh[:, m % 2, :], hf[:, m % 2, :]))
                    dve.wait_ge(dve_done, d)
                    nc.vector.tensor_tensor(hl[:, m % 2, :], hf[:, m % 2, :], hh[:, m % 2, :].bitcast(F32), ALU.subtract
                                            ).then_inc(h_split, 1)
                    if v_next and m in (1, 2):
                        for a in range(2):
                            mask_q(n + 1, m - 1, a)
                if v_next:
                    y_ready = add_b2(n)
                dve.wait_ge(dve_done, y_ready)
                dve.wait_ge(acc_ready, T_READY * n + 5)
                for a in range(2):
                    to = xn2[:, 2 * a:2 * a + 2, :]
                    nc.vector.tensor_tensor(to, acc[a][:].rearrange("p (m c) -> p m c", c=D),
                                            alpha2[:].unsqueeze(1).to_broadcast([P, 2, D]), ALU.mult
                                            ).then_inc(acc_free[a], 1)
                    dve.wait_ge(acc_free[a], T_FREE * n + 4)
                    nc.vector.tensor_tensor(to, to, y[:, 2 * a:2 * a + 2, :], ALU.add).then_inc(out_ready, 1)

            def signs(raw, sign, below):
                c = done(nc.vector.tensor_scalar(below, raw, 0.0, None, ALU.is_lt))
                dve.wait_ge(dve_done, c)
                c = done(nc.vector.scalar_tensor_tensor(sign, raw, 0.0, below, ALU.is_gt, ALU.subtract))
                dve.wait_ge(dve_done, c)

            def signs_w2(half):
                signs(w2t_raw[:, half, :], w2_sign[:, half * ST:(half + 1) * ST, :].rearrange("p a n -> p (a n)"),
                      probs[:, 2, :])

            nc.vector.memset(mean_w[:], 1.0 / HID).then_inc(mean_w_set, 1)
            done(nc.vector.memset(zero[:], 0.0))
            nc.vector.memset(v_aug[:, :, 0, :, 16:32], 1.0).then_inc(acc_free[0], 1)
            nc.vector.memset(v_aug[:, :, 1, :, 0:16], 1.0).then_inc(acc_free[1], 1)
            norm_x(0, 1)
            copy_x(0, first=True)
            dve.wait_ge(const_loaded, 48)
            lo_k(0, 0)
            lo_q(0)
            dve.wait_ge(w2_loaded, 16)
            signs_w2(0)
            lo_k(0, 1)
            dve.wait_ge(wv_loaded, 32)
            take_v(0, 0)
            signs_w2(1)
            nc.vector.memset(row_max[:], 0.0).then_inc(w2_used, 1)
            take_v(0, 1)

            mask_pairs(0, 0)
            for half in range(2):
                dve.wait_ge(bank_ready, half + 1)
                nc.vector.tensor_copy(alpha2[:, half * P:(half + 1) * P], bank[half][:, 0:P]).then_inc(bank_free[half], 1)
                dve.wait_ge(bank_free[half], 1)
            dve.wait_ge(ffn_loaded, 16 * 7)
            for half, raw in enumerate((hf, attnT)):
                c = done(nc.vector.tensor_reduce(alpha1[:, half * ST:(half + 1) * ST],
                                                 raw[:].rearrange("p a (b d) -> p (a b) d", d=D),
                                                 AX.X, ALU.add, apply_absolute_value=True))
            dve.wait_ge(dve_done, c)
            done(nc.vector.tensor_scalar(alpha1[:], alpha1[:], 1.0 / D, None, ALU.mult))
            for half in range(2):
                signs(stage[:, half, :], w1_sign[:, half, :], xn2[:].rearrange("p m c -> p (m c)"))
            nc.vector.memset(dve_idle, 0.0).then_inc(signs_ready, 1)

            def fast_batch(n, last):
                used = (A_USES + B_USES) * n + (A_USES + B_USES)
                mask_pairs(n, 2)
                residual(n)
                even = take_even(n, 0)
                mask_pairs(n, 4)
                count_mask(n, 0)
                if not last:
                    norm_x(n + 1, 2 * n + 2)
                take_odd(n, 0, even)
                mask_pairs(n, 6)
                count_mask(n, 1)
                check_sums(n, 0)
                even = take_even(n, 1)
                if not last:
                    copy_x(used)
                take_odd(n, 1, even, 2 if last else 1)
                if last:
                    check_sums(n, 1)
                    check_attention(n)
                else:
                    stage_a(n + 1)
                stage_o(n, 2 * n + (2 if last else 3))
                stage_f(n, used_before_f(n, last), None if last else used)
                if not last:
                    check_sums(n, 1)
                    check_attention(n)

            counted_loop(NB - 1, FAST_DONE, lambda n: fast_batch(n, False))
            fast_batch(NB - 1, True)

            mask_found = found[:, :, 0:2]
            good_found = found[:, :, 2:8]
            c = done(nc.vector.tensor_reduce(bad, mask_found, AX.XY, ALU.add))
            c = done(nc.vector.tensor_reduce(bad2, good_found, AX.XY, ALU.add))
            dve.wait_ge(dve_done, c)
            c = done(nc.vector.tensor_scalar(bad2, bad2, -1.0, float(NB * 6 * S), ALU.mult, ALU.add))
            dve.wait_ge(dve_done, c)
            nc.vector.tensor_tensor(bad, bad, bad2, ALU.add).then_inc(bad_ready, 1)
            dve.wait_ge(bad_summed, 1)
            c = done(nc.vector.tensor_scalar(bad_all, bank[0][:, 0:1], 0.0, None, ALU.not_equal))
            dve.wait_ge(dve_done, c)
            nc.vector.tensor_copy(flag[:], bad_all).then_inc(flag_ready, 1)
            dve.wait_ge(flag_ready, 1)

            def exact_batch(i):
                n = i + NB
                norm_x(n, 2 * i + 2 * NB + 1)
                used = (A_USES + X_USES) * i + (A_USES + B_USES) * NB
                copy_x(used)
                stage_a(n)
                take_v(used, 0)
                take_v(used, 1)
                residual(n)
                dve.wait_ge(mask_loaded, 32 * i + 32 * NB + 32)
                for g in range(NG):
                    dve.wait_ge(stack_ready[g], STACK * n + STACK)
                used = (A_USES + X_USES) * i + ((A_USES + B_USES) * NB + A_USES)
                for hd in range(NH):
                    if hd % 2 == 0:
                        for a in range(2):
                            mask_q(n, hd // 2, a)
                    for qi in range(ST):
                        k = hd * ST + qi
                        dve.wait_ge(slot_ready, used + 2 * k + 1)
                        nc.vector.scalar_tensor_tensor(probs[:, 0, :], slot[0][:], SCALE,
                                                       (stage, probs)[qi // 2][:, qi % 2 + 2 * (qi // 2), :],
                                                       ALU.mult, ALU.add).then_inc(slot_free[0], 1)
                        dve.wait_ge(slot_free[0], SLOT_X[0] * i + (SLOT_N[0] * NB + SLOT_A[0] + k + 1))
                        nc.vector.tensor_reduce(row_max[:], probs[:, 0, :], AX.X, ALU.max, negate=True
                                                ).then_inc(max_ready, 1)
                        dve.wait_ge(slot_ready, used + 2 * k + 2)
                        nc.vector.tensor_copy(probsT[:, :, qi * P:(qi + 1) * P],
                                              slot[1][:].rearrange("p (k q) -> p k q", q=P)).then_inc(slot_free[1], 1)
                    g, h = divmod(hd, GH)
                    if h == GH - 1:
                        if g % 2 == 0:
                            even = take_even(n, g // 2)
                        else:
                            take_odd(n, g // 2, even)
                stage_o(n, 2 * i + 2 * NB + 2)
                stage_f(n, SLOT_X[0] * i + (SLOT_N[0] * NB + SLOT_A[0] + X_USES // 2), None)

            with dve.If(dve.value_load(flag[0:1, 0:1]) != 0):
                counted_loop(NB, EXACT_DONE, exact_batch)




def _rows(w):
    return np.ascontiguousarray(w.reshape(-1, P, w.shape[1]).transpose(1, 0, 2))


def kernel(**inputs):
    import concourse.bacc as _bacc
    from concourse.bass_utils import run_bass_kernel_spmd as _run

    a = {k: np.asarray(v) for k, v in inputs.items()}
    f = lambda name: a["L0_" + name]
    tile, col, par, ch = np.meshgrid(np.arange(2), np.arange(4), np.arange(2), np.arange(DH), indexing="ij")
    attn_order = (DH * (GH * (2 * tile + par) + col) + ch).reshape(-1)
    par, half, col, ch = np.meshgrid(np.arange(2), np.arange(2), np.arange(4), np.arange(DH), indexing="ij")
    v_order = (DH * (GH * (2 * half + par) + col) + ch).reshape(-1)
    tile, group, odd, ch = np.meshgrid(np.arange(2), np.arange(NG), np.arange(2), np.arange(DH), indexing="ij")
    qk_order = (DH * (GH * group + 2 * tile + odd) + ch).reshape(-1)
    row = lambda v: np.ascontiguousarray(np.broadcast_to(v[None, :], (P, v.shape[0])))
    col_ = lambda v: np.ascontiguousarray(v.reshape(-1, P).T)
    w1, w2 = f("ffn_w1"), f("ffn_w2")
    lane = np.arange(P) % 32 < 16
    arrays = {
        "x": a["x"], "ctx_t": np.ascontiguousarray(a["ctx_1024"].transpose(0, 2, 1)), "mask": a["mask_BxSxS2_ff0"],
        "wq_t": _rows(f("xattn_Wq").T[:, qk_order]), "wk_t": _rows(f("xattn_Wk").T[:, qk_order]),
        "wv_t": _rows(f("xattn_Wv").T[:, v_order]),
        "wo_t": _rows(f("xattn_Wo").T[attn_order]), "bq": col_(f("xattn_bq")[qk_order]), "bk": col_(f("xattn_bk")[qk_order]),
        "bv_row": row(f("xattn_bv")[v_order]), "bo_row": row(f("xattn_bo")),
        "w1": _rows(w1).reshape(P, -1), "w1_t": _rows(w1.T), "w2_t": _rows(w2.T).reshape(P, -1),
        "b1": col_(f("ffn_b1")), "b2_row": row(f("ffn_b2")),
        "ident": np.eye(P, dtype=np.float32), "halves": np.stack([lane, ~lane], 1).astype(np.float32),
    }
    nc = _bacc.Bacc("TRN2", target_bir_lowering=False, num_devices=1)
    args = [nc.dram_tensor("in_" + n, v.shape, F32, kind="ExternalInput").ap() for n, v in arrays.items()]
    out = nc.dram_tensor("out", (NB, S, D), F32, kind="ExternalOutput").ap()
    layer(nc, *args, out)
    r = _run(nc, [{"in_" + n: v for n, v in arrays.items()}], core_ids=[0])
    return r.results[0]["out"]
```
